# Optimizing a Trainium2 kernel written in Bass

```python
import numpy as np
import jax
import jax.numpy as jnp

def _softmax(x, axis=-1):
    return jax.nn.softmax(x, axis=axis)

def _gelu(x):
    return jax.nn.gelu(x, approximate=True)

def _silu(x):
    return jax.nn.silu(x)

def _sigmoid(x):
    return jax.nn.sigmoid(x)

def _layernorm(x, axis=-1, eps=1e-05):
    m = jnp.mean(x, axis=axis, keepdims=True)
    v = jnp.var(x, axis=axis, keepdims=True)
    return (x - m) / jnp.sqrt(v + eps)

def _scatter_add(tgt, idx, src, axis=0):
    return tgt.at[idx].add(src)

def _segment_sum(src, seg, n):
    return jax.ops.segment_sum(src, seg, n)
kernel_name = 'mk_recurrent_d2_jaxref_r8_415e50'

def setup_inputs(seed: int=0):
    np.random.seed(seed)
    _w = jnp.asarray

    def _L0_attn_setup():
        import jax, jax.numpy as jnp
        import numpy as np
        B, S, D = (4, 512, 128)

        def _scan_causal(x_scan, a):

            def step(h, inp):
                a_t, x_t = inp
                h = a_t * h + x_t
                return (h, h)
            h0 = jnp.zeros(x_scan.shape[::2], dtype=x_scan.dtype)
            xs = (jnp.swapaxes(a, 0, 1), jnp.swapaxes(x_scan, 0, 1))
            _, out = jax.lax.scan(step, h0, xs)
            return jnp.swapaxes(out, 0, 1)
        key = jax.random.key(seed)
        ks = jax.random.split(key, 4)
        scale = 1.0 / np.sqrt(D)
        x = jax.random.normal(ks[0], (B, S, D), dtype=jnp.float32)
        Wg = jax.random.normal(ks[1], (D, D), dtype=jnp.float32) * scale
        Wv = jax.random.normal(ks[2], (D, D), dtype=jnp.float32) * scale
        Wd = jax.random.normal(ks[3], (D, D), dtype=jnp.float32) * scale
        bg = jnp.zeros((D,), dtype=jnp.float32)
        bv = jnp.zeros((D,), dtype=jnp.float32)
        bd = jnp.ones((D,), dtype=jnp.float32)
        return {'x': x, 'Wg': Wg, 'bg': bg, 'Wv': Wv, 'bv': bv, 'Wd': Wd, 'bd': bd}
    _L0_attn_in = _L0_attn_setup()

    def _L0_ffn_setup():
        import jax, jax.numpy as jnp
        import numpy as np
        D_MODEL = 128
        FFN_DIM = 256
        NUM_EXPERTS = 8
        NUM_GROUPS = 4
        EXPERTS_PER_GROUP = NUM_EXPERTS // NUM_GROUPS
        TOP_K = 2
        GROUPS_TOP_K = 1
        EPS = 1e-09

        def _topk_normalized(scores, k):
            vals, idx = jax.lax.top_k(scores, k)
            vals = vals / (jnp.sum(vals, axis=-1, keepdims=True) + EPS)
            return (vals, idx)
        key = jax.random.key(seed)
        ks = jax.random.split(key, 6)
        B, S = (2, 128)
        x = jax.random.normal(ks[0], (B, S, D_MODEL), dtype=jnp.float32)
        sd = 0.02
        macro_w = jax.random.normal(ks[1], (D_MODEL, NUM_GROUPS), dtype=jnp.float32) * sd
        micro_w = jax.random.normal(ks[2], (NUM_GROUPS, D_MODEL, EXPERTS_PER_GROUP), dtype=jnp.float32) * sd
        gate_w = jax.random.normal(ks[3], (NUM_EXPERTS, D_MODEL, FFN_DIM), dtype=jnp.float32) * sd
        up_w = jax.random.normal(ks[4], (NUM_EXPERTS, D_MODEL, FFN_DIM), dtype=jnp.float32) * sd
        down_w = jax.random.normal(ks[5], (NUM_EXPERTS, FFN_DIM, D_MODEL), dtype=jnp.float32) * sd
        return {'x': x, 'macro_w': macro_w, 'micro_w': micro_w, 'gate_w': gate_w, 'up_w': up_w, 'down_w': down_w}
    _L0_ffn_in = _L0_ffn_setup()

    def _L1_attn_setup():
        import jax, jax.numpy as jnp
        import numpy as np
        EPS = 1e-06
        CHUNK = 128

        def _feature_map(x):
            return jax.nn.elu(x) + 1.0

        def _linear_attention(q, k, v):
            B, T, D = q.shape
            C = CHUNK
            N = T // C
            qc = q.reshape(B, N, C, D).transpose(1, 0, 2, 3)
            kc = k.reshape(B, N, C, D).transpose(1, 0, 2, 3)
            vc = v.reshape(B, N, C, D).transpose(1, 0, 2, 3)
            mask = jnp.tril(jnp.ones((C, C), bool))

            def step(carry, inp):
                key_sum, kv_sum = carry
                qi, ki, vi = inp
                A = jnp.einsum('bcd,bsd->bcs', qi, ki)
                A = jnp.where(mask, A, 0.0)
                num = jnp.einsum('bcs,bse->bce', A, vi) + jnp.einsum('bcd,bde->bce', qi, kv_sum)
                den = A.sum(-1) + jnp.einsum('bcd,bd->bc', qi, key_sum) + EPS
                out_i = num / den[..., None]
                key_sum = key_sum + ki.sum(1)
                kv_sum = kv_sum + jnp.einsum('bcd,bce->bde', ki, vi)
                return ((key_sum, kv_sum), out_i)
            init = (jnp.zeros((B, D), q.dtype), jnp.zeros((B, D, D), q.dtype))
            (key_sum, kv_sum), out = jax.lax.scan(step, init, (qc, kc, vc))
            out = out.transpose(1, 0, 2, 3).reshape(B, T, D)
            return (out, key_sum, kv_sum)

        def _reference_tuple_inner(chunk, Wq, bq, Wk, bk, Wv, bv, Wo, bo):
            q = _feature_map(chunk @ Wq.T + bq)
            k = _feature_map(chunk @ Wk.T + bk)
            v = chunk @ Wv.T + bv
            attn, key_sum, kv_sum = _linear_attention(q, k, v)
            out = attn @ Wo.T + bo
            return (out, key_sum, kv_sum)
        key = jax.random.key(seed)
        ks = jax.random.split(key, 9)
        B, T, D = (4, 256, 128)
        s = 1.0 / np.sqrt(D)
        f32 = jnp.float32
        return {'chunk': jax.random.normal(ks[0], (B, T, D), f32), 'Wq': jax.random.normal(ks[1], (D, D), f32) * s, 'bq': jnp.zeros((D,), f32), 'Wk': jax.random.normal(ks[2], (D, D), f32) * s, 'bk': jnp.zeros((D,), f32), 'Wv': jax.random.normal(ks[3], (D, D), f32) * s, 'bv': jnp.zeros((D,), f32), 'Wo': jax.random.normal(ks[4], (D, D), f32) * s, 'bo': jnp.zeros((D,), f32)}
    _L1_attn_in = _L1_attn_setup()

    def _L1_ffn_setup():
        import jax, jax.numpy as jnp
        import numpy as np
        DIM = 128
        HIDDEN = 128
        NUM_EXPERTS = 8
        TOP_K = 2
        key = jax.random.key(seed)
        ks = jax.random.split(key, 8)
        std = 0.02
        x = jax.random.normal(ks[0], (2, 128, DIM), dtype=jnp.float32)
        gate_w = jax.random.normal(ks[1], (NUM_EXPERTS, DIM), dtype=jnp.float32) * std
        w1 = jax.random.normal(ks[2], (NUM_EXPERTS, DIM, HIDDEN), dtype=jnp.float32) * std
        w2 = jax.random.normal(ks[3], (NUM_EXPERTS, HIDDEN, DIM), dtype=jnp.float32) * std
        w3 = jax.random.normal(ks[4], (NUM_EXPERTS, DIM, HIDDEN), dtype=jnp.float32) * std
        w1s = jax.random.normal(ks[5], (1, DIM, HIDDEN), dtype=jnp.float32) * std
        w2s = jax.random.normal(ks[6], (1, HIDDEN, DIM), dtype=jnp.float32) * std
        w3s = jax.random.normal(ks[7], (1, DIM, HIDDEN), dtype=jnp.float32) * std
        return {'x': x, 'gate_w': gate_w, 'w1': w1, 'w2': w2, 'w3': w3, 'w1s': w1s, 'w2s': w2s, 'w3s': w3s}
    _L1_ffn_in = _L1_ffn_setup()
    _d = {'L0_attn_x': _L0_attn_in['x'], 'L0_attn_Wg': _L0_attn_in['Wg'], 'L0_attn_bg': _L0_attn_in['bg'], 'L0_attn_Wv': _L0_attn_in['Wv'], 'L0_attn_bv': _L0_attn_in['bv'], 'L0_attn_Wd': _L0_attn_in['Wd'], 'L0_attn_bd': _L0_attn_in['bd'], 'L0_ffn_macro_w': _L0_ffn_in['macro_w'], 'L0_ffn_micro_w': _L0_ffn_in['micro_w'], 'L0_ffn_gate_w': _L0_ffn_in['gate_w'], 'L0_ffn_up_w': _L0_ffn_in['up_w'], 'L0_ffn_down_w': _L0_ffn_in['down_w'], 'L1_attn_Wq': _L1_attn_in['Wq'], 'L1_attn_bq': _L1_attn_in['bq'], 'L1_attn_Wk': _L1_attn_in['Wk'], 'L1_attn_bk': _L1_attn_in['bk'], 'L1_attn_Wv': _L1_attn_in['Wv'], 'L1_attn_bv': _L1_attn_in['bv'], 'L1_attn_Wo': _L1_attn_in['Wo'], 'L1_attn_bo': _L1_attn_in['bo'], 'L1_ffn_gate_w': _L1_ffn_in['gate_w'], 'L1_ffn_w1': _L1_ffn_in['w1'], 'L1_ffn_w2': _L1_ffn_in['w2'], 'L1_ffn_w3': _L1_ffn_in['w3'], 'L1_ffn_w1s': _L1_ffn_in['w1s'], 'L1_ffn_w2s': _L1_ffn_in['w2s'], 'L1_ffn_w3s': _L1_ffn_in['w3s']}
    _x0 = _d['L0_attn_x']
    _d['L0_attn_x'] = jax.random.normal(jax.random.fold_in(jax.random.key(seed), 1), (8, 512, 128), dtype=_x0.dtype)
    del _x0
    return _d

def reference(L0_attn_x, L0_attn_Wg, L0_attn_bg, L0_attn_Wv, L0_attn_bv, L0_attn_Wd, L0_attn_bd, L0_ffn_macro_w, L0_ffn_micro_w, L0_ffn_gate_w, L0_ffn_up_w, L0_ffn_down_w, L1_attn_Wq, L1_attn_bq, L1_attn_Wk, L1_attn_bk, L1_attn_Wv, L1_attn_bv, L1_attn_Wo, L1_attn_bo, L1_ffn_gate_w, L1_ffn_w1, L1_ffn_w2, L1_ffn_w3, L1_ffn_w1s, L1_ffn_w2s, L1_ffn_w3s):

    def _L0_attn_ref(x, Wg, bg, Wv, bv, Wd, bd):
        import jax, jax.numpy as jnp
        import numpy as np
        B, S, D = (4, 512, 128)

        def _scan_causal(x_scan, a):

            def step(h, inp):
                a_t, x_t = inp
                h = a_t * h + x_t
                return (h, h)
            h0 = jnp.zeros(x_scan.shape[::2], dtype=x_scan.dtype)
            xs = (jnp.swapaxes(a, 0, 1), jnp.swapaxes(x_scan, 0, 1))
            _, out = jax.lax.scan(step, h0, xs)
            return jnp.swapaxes(out, 0, 1)
        g = jnp.einsum('bsd,ed->bse', x, Wg) + bg
        v = jnp.einsum('bsd,ed->bse', x, Wv) + bv
        d = jnp.einsum('bsd,ed->bse', x, Wd) + bd
        x_scan = jax.nn.sigmoid(g) * jnp.tanh(v)
        a = 0.001 + 0.998 * jax.nn.sigmoid(d)
        return _scan_causal(x_scan, a)

    def _L0_ffn_ref(x, macro_w, micro_w, gate_w, up_w, down_w):
        import jax, jax.numpy as jnp
        import numpy as np
        D_MODEL = 128
        FFN_DIM = 256
        NUM_EXPERTS = 8
        NUM_GROUPS = 4
        EXPERTS_PER_GROUP = NUM_EXPERTS // NUM_GROUPS
        TOP_K = 2
        GROUPS_TOP_K = 1
        EPS = 1e-09

        def _topk_normalized(scores, k):
            vals, idx = jax.lax.top_k(scores, k)
            vals = vals / (jnp.sum(vals, axis=-1, keepdims=True) + EPS)
            return (vals, idx)
        B, S, D = x.shape
        T = B * S
        xf = x.reshape(T, D)
        macro_scores = jax.nn.sigmoid(xf @ macro_w)
        mv, mi = _topk_normalized(macro_scores, GROUPS_TOP_K)
        macro_full = jnp.sum(jax.nn.one_hot(mi, NUM_GROUPS, dtype=xf.dtype) * mv[..., None], axis=1)
        micro_scores = jax.nn.sigmoid(jnp.einsum('td,gde->tge', xf, micro_w))
        uv, ui = _topk_normalized(micro_scores, TOP_K)
        micro_full = jnp.sum(jax.nn.one_hot(ui, EXPERTS_PER_GROUP, dtype=xf.dtype) * uv[..., None], axis=2)
        w = (macro_full[:, :, None] * micro_full).reshape(T, NUM_EXPERTS)
        gate = jax.nn.silu(jnp.einsum('td,edf->tef', xf, gate_w))
        up = jnp.einsum('td,edf->tef', xf, up_w)
        h = gate * up
        out = jnp.einsum('te,tef,efd->td', w, h, down_w)
        return out.reshape(B, S, D)

    def _L1_attn_ref(chunk, Wq, bq, Wk, bk, Wv, bv, Wo, bo):
        import jax, jax.numpy as jnp
        import numpy as np
        EPS = 1e-06
        CHUNK = 128

        def _feature_map(x):
            return jax.nn.elu(x) + 1.0

        def _linear_attention(q, k, v):
            B, T, D = q.shape
            C = CHUNK
            N = T // C
            qc = q.reshape(B, N, C, D).transpose(1, 0, 2, 3)
            kc = k.reshape(B, N, C, D).transpose(1, 0, 2, 3)
            vc = v.reshape(B, N, C, D).transpose(1, 0, 2, 3)
            mask = jnp.tril(jnp.ones((C, C), bool))

            def step(carry, inp):
                key_sum, kv_sum = carry
                qi, ki, vi = inp
                A = jnp.einsum('bcd,bsd->bcs', qi, ki)
                A = jnp.where(mask, A, 0.0)
                num = jnp.einsum('bcs,bse->bce', A, vi) + jnp.einsum('bcd,bde->bce', qi, kv_sum)
                den = A.sum(-1) + jnp.einsum('bcd,bd->bc', qi, key_sum) + EPS
                out_i = num / den[..., None]
                key_sum = key_sum + ki.sum(1)
                kv_sum = kv_sum + jnp.einsum('bcd,bce->bde', ki, vi)
                return ((key_sum, kv_sum), out_i)
            init = (jnp.zeros((B, D), q.dtype), jnp.zeros((B, D, D), q.dtype))
            (key_sum, kv_sum), out = jax.lax.scan(step, init, (qc, kc, vc))
            out = out.transpose(1, 0, 2, 3).reshape(B, T, D)
            return (out, key_sum, kv_sum)

        def _reference_tuple_inner(chunk, Wq, bq, Wk, bk, Wv, bv, Wo, bo):
            q = _feature_map(chunk @ Wq.T + bq)
            k = _feature_map(chunk @ Wk.T + bk)
            v = chunk @ Wv.T + bv
            attn, key_sum, kv_sum = _linear_attention(q, k, v)
            out = attn @ Wo.T + bo
            return (out, key_sum, kv_sum)
        return _reference_tuple_inner(chunk, Wq, bq, Wk, bk, Wv, bv, Wo, bo)[0]

    def _L1_ffn_ref(x, gate_w, w1, w2, w3, w1s, w2s, w3s):
        import jax, jax.numpy as jnp
        import numpy as np
        DIM = 128
        HIDDEN = 128
        NUM_EXPERTS = 8
        TOP_K = 2
        bs, slen, dim = x.shape
        xt = x.reshape(bs * slen, dim)
        logits = xt @ gate_w.T
        scores = jax.nn.softmax(logits.astype(jnp.float32), axis=1).astype(x.dtype)
        top_scores, sel = jax.lax.top_k(scores, TOP_K)
        sel_flat = sel.reshape(-1)
        order = jnp.argsort(sel_flat, stable=True)
        top_scores_sorted = top_scores.reshape(-1)[order]
        token_idx = order // TOP_K
        eid = sel_flat[order]
        routed_in = xt[token_idx] * top_scores_sorted[:, None]
        out_routed = jnp.zeros_like(routed_in)
        for e in range(NUM_EXPERTS):
            m = (eid == e)[:, None]
            xe = jnp.where(m, routed_in, 0.0)
            h = jax.nn.silu(xe @ w1[e]) * (xe @ w3[e])
            out_routed = out_routed + jnp.where(m, h @ w2[e], 0.0)
        hs = jax.nn.silu(xt @ w1s[0]) * (xt @ w3s[0])
        out = hs @ w2s[0]
        out = out.at[token_idx].add(out_routed)
        return out.reshape(bs, slen, dim)
    x = L0_attn_x
    xn = _layernorm(x, axis=-1)
    s = _L0_attn_ref(xn, L0_attn_Wg, L0_attn_bg, L0_attn_Wv, L0_attn_bv, L0_attn_Wd, L0_attn_bd)
    g = _silu(_L0_ffn_ref(xn, L0_ffn_macro_w, L0_ffn_micro_w, L0_ffn_gate_w, L0_ffn_up_w, L0_ffn_down_w))
    x = x + s * g
    xn = _layernorm(x, axis=-1)
    s = _L1_attn_ref(xn, L1_attn_Wq, L1_attn_bq, L1_attn_Wk, L1_attn_bk, L1_attn_Wv, L1_attn_bv, L1_attn_Wo, L1_attn_bo)
    g = _silu(_L1_ffn_ref(xn, L1_ffn_gate_w, L1_ffn_w1, L1_ffn_w2, L1_ffn_w3, L1_ffn_w1s, L1_ffn_w2s, L1_ffn_w3s))
    x = x + s * g
    return x

_drawn_inputs = setup_inputs


def setup_inputs(seed=0):
    import zlib

    import numpy as np

    out = dict(_drawn_inputs(seed))
    spreads = {'L0_attn_bg': (0.0, 0.8),
     'L0_attn_bv': (0.0, 0.8),
     'L0_attn_bd': (1.0, 0.6),
     'L1_attn_bq': (0.0, 0.8),
     'L1_attn_bk': (0.0, 0.8),
     'L1_attn_bv': (0.0, 0.8),
     'L1_attn_bo': (0.0, 0.8)}
    factors = {'L0_attn_Wg': 8.0,
     'L0_attn_Wv': 8.0,
     'L0_attn_Wd': 8.0,
     'L0_ffn_macro_w': 8.0,
     'L0_ffn_micro_w': 8.0,
     'L0_ffn_gate_w': 8.0,
     'L0_ffn_up_w': 8.0,
     'L0_ffn_down_w': 8.0,
     'L1_attn_Wq': 8.0,
     'L1_attn_Wk': 8.0,
     'L1_attn_Wv': 8.0,
     'L1_attn_Wo': 8.0,
     'L1_ffn_gate_w': 8.0,
     'L1_ffn_w1': 8.0,
     'L1_ffn_w2': 8.0,
     'L1_ffn_w3': 8.0,
     'L1_ffn_w1s': 8.0,
     'L1_ffn_w2s': 8.0,
     'L1_ffn_w3s': 8.0}
    for name, (base, spread) in spreads.items():
        noise = np.random.default_rng([zlib.crc32(name.encode()), seed]).standard_normal(out[name].shape)
        drawn = base * np.exp(spread * noise) if base else spread * noise
        out[name] = jnp.asarray(drawn.astype(out[name].dtype))
    for name, factor in factors.items():
        out[name] = (out[name] * factor).astype(out[name].dtype)
    return out
```

```python
from contextlib import ExitStack

import concourse.bass as bass
from concourse import mybir

ALU = mybir.AluOpType
ACT = mybir.ActivationFunctionType
AX_X = mybir.AxisListType.X
F32 = mybir.dt.float32
I32 = mybir.dt.int32
U32 = mybir.dt.uint32

P = 128
SEQS = 8
TPS = 4
SEQ = TPS * P
TILES = SEQS * TPS
HALVES = 2
HT = TILES // HALVES
HSEQ = SEQS // HALVES
GROUPS = 4
EPG = 2
F0 = 256
FT = HT + GROUPS - 1
SORTED = HALVES * FT
ROW = P + EPG
HC = EPG * F0 // P
E1 = 8
PAIRS = E1 // 2
UNITS = PAIRS + 1
USEQ = UNITS * TPS
NR = GROUPS + GROUPS * EPG
LN_EPS = 1e-5
TOPK_EPS = 1e-9
ATT_EPS = 1e-6
MAGIC = float(1 << 23)

C_ID, C_LOWER, C_CAUSAL, C_ONES = (i * P for i in range(4))
C_FALL = C_CAUSAL + SEQ
C_TILE = C_FALL + E1
CONSTS = C_TILE + FT


def gated_recurrent_moe_two_layers(
    nc, x, consts, router0, attn0_w, attn0_b, gate_up0, down0,
    attn1_w, attn1_b, wo1, bo1, w13, w2, out,
):
    ctx = ExitStack()
    with ctx:
        def sb(name, shape, dt=F32):
            return ctx.enter_context(nc.sbuf_tensor(name, shape, dt))

        def sem(name):
            return ctx.enter_context(nc.semaphore(name))

        sorted_rows = nc.dram_tensor("sorted_rows", [SORTED * P, ROW], F32, kind="Internal").ap()
        sorted_y = nc.dram_tensor("sorted_y", [SORTED * P, P], F32, kind="Internal").ap()
        x_t = x.rearrange("b (t p) d -> b p t d", p=P)
        out_t = out.rearrange("b (t p) d -> (b t) p d", p=P)
        rows_t = sorted_rows.rearrange("(n p) c -> n p c", p=P)
        y_t = sorted_y.rearrange("(n p) c -> n p c", p=P)

        ps = ctx.enter_context(nc.psum_tensor("ps", [P, 8, 512], F32))

        cst = sb("cst", [P, CONSTS])
        ident = cst[:, C_ID:C_ID + P]
        lower = cst[:, C_LOWER:C_LOWER + P]
        ones = cst[:, C_ONES:C_ONES + P]
        fall = cst[:, C_FALL:C_FALL + E1]
        r0 = sb("r0", [P, NR])
        a0w = sb("a0w", [P, 3 * P])
        a0b = sb("a0b", [P, 3])
        a0bh = sb("a0bh", [P, 3])
        gu0 = sb("gu0", [P, GROUPS * 2 * EPG * F0])
        dn0 = sb("dn0", [P, GROUPS * HC * P])
        a1w = sb("a1w", [P, 3 * P])
        a1b = sb("a1b", [P, 3])
        a1b1 = sb("a1b1", [P, 2])
        wo = sb("wo", [P, P])
        bo = sb("bo", [P, P])
        w13s = sb("w13s", [P, (2 * E1 + 2) * P])
        w2s = sb("w2s", [P, (E1 + 1) * P])
        vg_w = sb("vg_w", [P, P + E1])
        bv_wo = sb("bv_wo", [P, P])
        bv_cols = sb("bv_cols", [P, P])
        minus_half = sb("minus_half", [P, 2 * TPS])
        zero_rows = sb("zero_rows", [P, 2 * ROW])
        warm = sb("warm", [P, 1])

        xa = sb("xa", [P, TILES, P])
        xnT = sb("xnT", [P, SEQS * SEQ])
        rows = sb("rows", [P, TILES, ROW])
        slot = sb("slot", [P, TILES], U32)
        group = sb("group", [1, SORTED], I32)
        sT = sb("sT", [P, TILES, P])
        ya = xnT[:, :].rearrange("p (t d) -> p t d", d=P)

        st = sb("st", [P, HT, 6])
        mv = sb("mv", [P, HT, 2])
        var = sb("var", [P, HT])
        rstd = sb("rstd", [P, HT])
        xnb = sb("xnb", [P, HT, P])
        lgT = sb("lgT", [NR, 2, SEQ])
        th_r = sb("th_r", [P, HT, NR])
        sc_r = sb("sc_r", [P, HT, NR])
        best = sb("best", [P, HT])
        best_e = sb("best_e", [P, HT])
        mfac = sb("mfac", [P, HT])
        ohg = sb("ohg", [P, HT, GROUPS])
        cum = sb("cum", [P, GROUPS, HT])
        cnt = sb("cnt", [P, GROUPS])
        tot = sb("tot", [P, 2 * GROUPS])
        ntile = sb("ntile", [P, GROUPS])
        ends = sb("ends", [P, GROUPS])
        base = sb("base", [P, GROUPS])
        where = sb("where", [P, GROUPS, HT])
        slot_f = sb("slot_f", [P, HT])
        group_f = sb("group_f", [1, FT])
        past = sb("past", [P, FT, GROUPS - 1])
        usum = sb("usum", [P, HT, GROUPS])
        uw = sb("uw", [P, HT, GROUPS, EPG])

        tg = sb("tg", [P, 2, SEQ])
        tv = sb("tv", [P, 2, SEQ])
        td = sb("td", [P, 2, SEQ])
        scan = sb("scan", [P, 2, SEQ])

        srow = sb("srow", [P, 2, ROW])
        sw = sb("sw", [P, 2, EPG])
        sxT = sb("sxT", [P, 2, P])
        th0 = sb("th0", [P, 2, 512])
        dummy = sb("first_act", [P, 2])
        h0 = sb("h0", [P, 2, 512])
        h0T = sb("h0T", [P, 2, 512])
        y0 = sb("y0", [P, 2, P])

        thy = sb("thy", [P, SEQ])
        gy = sb("gy", [P, SEQ])
        st1 = sb("st1", [P, TPS, 6])
        mv1 = sb("mv1", [P, TPS, 2])
        var1 = sb("var1", [P, TPS])
        rstd1 = sb("rstd1", [P, TPS])
        xn1 = sb("xn1", [P, TPS, P])
        xn1T = sb("xn1T", [P, SEQ])
        xc = sb("xc", [P, TPS, P])
        expq, linq = tg, tv
        qT = sb("qT", [P, SEQ])
        kT = sb("kT", [P, SEQ])
        vo = sb("vo", [P, TPS, P + 1])
        at = sb("at", [P, TPS, SEQ])
        lg = sb("lg", [P, TPS, E1])
        e1 = sb("e1", [P, TPS, E1])
        pr = sb("pr", [P, TPS, E1])
        rq = sb("rq", [P, TPS, E1])
        oh1 = sb("oh1", [P, TPS, E1])
        oh2 = sb("oh2", [P, TPS, E1])
        rm = sb("rm", [P, TPS])
        rs = sb("rs", [P, TPS])
        half_s = sb("half_s", [P, TPS, E1])
        half_s2 = sb("half_s2", [P, TPS, E1])
        den = sb("den", [P, TPS])
        s1 = sb("s1", [P, TPS, P])
        th1 = sb("th1", [P, 2, 2 * P])
        a1 = sb("a1", [P, 2, 2 * P])
        h1 = sb("h1", [P, 2, 2 * P])
        h1T = sb("h1T", [P, 2, 2 * P])
        thf = sb("thf", [P, 2, P])
        gf = sb("gf", [P, 2, P])
        of = sb("of", [P, 2, P])
        xo = sb("xo", [P, 2, P])

        names = """dummy_set warm x_in consts_in attn0_in attn1_in experts0_in experts1_in zeroed zero_tile pool_const
            chain vars rstds normed turned xnT_ready routed lgT_ready lg_turned scored rows_ready
            counted placed slots_ready group_ready bias0_ready bias1_ready
            rec_mm rec_act rec_x rec_scan rec_turned rec_out fused fused_out
            f_turned f_w f_xT f_gate f_up f_th f_a f_h f_hT f_hTs f_down f_y gathered
            c_chain c_th c_var c_rstd c_xn c_turned c_xT c_copy c_q c_k c_lin c_qkT
            c_v c_lg c_lgm c_exp c_scores c_a c_at c_num c_den c_s1
            m_gu m_th m_a m_h m_hT m_hTs m_y m_thf m_gf m_of m_xo""".split()
        s = {n: sem(n) for n in names}
        loaded = [sem(f"loaded{i}") for i in range(2)]
        y_stored = [sem(f"y_stored{i}") for i in range(2)]
        o_stored = [sem(f"o_stored{i}") for i in range(2)]

        def wait(eng, name, value):
            if not (isinstance(value, int) and value <= 0):
                eng.wait_ge(s[name] if isinstance(name, str) else name, value)

        FREE = 16
        scattered = [sem(f"scattered{h}") for h in range(HALVES)]

        def tile_of(tiles, n):
            return tiles[bass.ds(n, 1)].rearrange("o p c -> (o p) c")

        def seq_of(tiles, q):
            return tiles[:, bass.ds(q * TPS, TPS), :]

        def half_of(n, par):
            return (n - par) // 2

        block = ctx.enter_context(nc.Block())

        @block.sync
        def _(sp):
            for q in range(HSEQ):
                sp.dma_start(xa[:, TPS * q:TPS * (q + 1), :], x_t[q]).then_inc(s["x_in"], 16)
            sp.dma_start(cst[:, :], consts).then_inc(s["consts_in"], 16)
            sp.dma_start(r0[:, :], router0).then_inc(s["consts_in"], 16)
            sp.wait_ge(s["x_in"], 16 * HSEQ)
            for q in range(HSEQ, SEQS):
                sp.dma_start(xa[:, TPS * q:TPS * (q + 1), :], x_t[q]).then_inc(s["x_in"], 16)
            sp.dma_start(a0w[:, :], attn0_w).then_inc(s["attn0_in"], 16)
            sp.dma_start(a0b[:, :], attn0_b).then_inc(s["attn0_in"], 16)
            sp.wait_ge(s["zero_tile"], 1)
            sp.dma_start(sorted_rows.rearrange("(p n r) c -> p n (r c)", p=P, r=2),
                         zero_rows[:, :].unsqueeze(1).broadcast_to([P, SORTED // 2, 2 * ROW])).then_inc(s["zeroed"], 16)
            for to, src in ((a1w, attn1_w), (a1b, attn1_b), (wo, wo1), (bo, bo1)):
                sp.dma_start(to[:, :], src).then_inc(s["attn1_in"], 16)
            sp.dma_start(gu0[:, :], gate_up0).then_inc(s["experts0_in"], 16)
            sp.dma_start(dn0[:, :], down0).then_inc(s["experts0_in"], 16)
            sp.dma_start(vg_w[:, P:P + E1], w13[:, (2 * E1 + 2) * P:]).then_inc(s["experts1_in"], 16)
            sp.dma_start(w13s[:, :], w13[:, 0:(2 * E1 + 2) * P]).then_inc(s["experts1_in"], 16)
            sp.dma_start(w2s[:, :], w2).then_inc(s["experts1_in"], 16)

            def load(n, par):
                wait(sp, "f_turned", n - 1)
                wait(sp, "f_w", n - 1)
                sp.dma_start(srow[:, par, :], tile_of(rows_t, n)).then_inc(loaded[par], 16)

            def store(n, par):
                wait(sp, "f_y", n + 1)
                sp.dma_start(tile_of(y_t, n), y0[:, par, :]).then_inc(y_stored[par], 16)

            def load_and_store(i):
                for par in range(2):
                    load(2 * i + 2 + par, par)
                    store(2 * i + par, par)

            sp.wait_ge(scattered[0], 16 * HT)
            load(0, 0)
            load(1, 1)
            load_and_store(0)
            mid = (FT - 2) // 2
            with sp.Fori(1, mid) as i:
                load_and_store(i)
            sp.wait_ge(scattered[1], 16 * HT)
            with sp.Fori(mid, SORTED // 2 - 1) as i:
                load_and_store(i)
            for n in (SORTED - 2, SORTED - 1):
                store(n, n % 2)

            with sp.Fori(0, SEQS) as b:
                for t in range(TPS):
                    sp.wait_ge(s["m_xo"], b * TPS + t + 1)
                    sp.dma_start(tile_of(out_t, b * TPS + t), xo[:, t % 2, :]).then_inc(o_stored[t % 2], 16)
            for par in range(2):
                sp.wait_ge(o_stored[par], FREE + 16 * TILES // 2)
                sp.wait_ge(y_stored[par], FREE + 16 * SORTED // 2)

        @block.gpsimd
        def _(pool):
            pool.memset(minus_half[:, :], -0.5).then_inc(s["pool_const"], 1)
            pool.memset(zero_rows[:, :], 0.0).then_inc(s["zero_tile"], 1)
            pool.memset(vo[:, :, P:P + 1], 1.0).then_inc(s["pool_const"], 1)
            pool.wait_ge(s["pool_const"], 2)

            for i in range(2 * HALVES):
                pool.wait_ge(s["vars"], i + 1)
                if i >= 2:
                    pool.wait_ge(s["normed"], 2 * (i - 1))
                part = slice((i % 2) * 2 * TPS, (i % 2 + 1) * 2 * TPS)
                pool.tensor_tensor(rstd[:, part], var[:, part], minus_half[:, :], ALU.pow).then_inc(s["rstds"], 1)

            pool.wait_ge(s["zeroed"], 16)
            for h in range(HALVES):
                pool.wait_ge(s["slots_ready"], h + 1)
                pool.wait_ge(s["rows_ready"], HSEQ * (h + 1))
                for t in range(HT * h, HT * (h + 1)):
                    pool.indirect_dma_start(
                        sorted_rows, bass.IndirectOffsetOnAxis(ap=slot[:, t:t + 1], axis=0),
                        rows[:, t, :], None).then_inc(scattered[h], 16)

            def gather(b):
                if b % HSEQ == 0:
                    last = FT * (b // HSEQ + 1) - 1
                    for n in (last - 1, last):
                        pool.wait_ge(y_stored[n % 2], FREE + 16 * (n // 2 + 1))
                if b > 0:
                    pool.wait_ge(s["gathered"], 16 * TPS * b)
                for t in range(TPS * b, TPS * (b + 1)):
                    pool.indirect_dma_start(
                        ya[:, t, :], None, sorted_y[0:FT * P * (b // HSEQ + 1)],
                        bass.IndirectOffsetOnAxis(ap=slot[:, t:t + 1], axis=0)).then_inc(s["gathered"], 16)

            for b in range(HSEQ):
                gather(b)
            gather(HSEQ)
            for b in range(SEQS):
                pool.wait_ge(s["c_var"], b + 1)
                pool.tensor_tensor(rstd1[:, :], var1[:, :], minus_half[:, 0:TPS], ALU.pow).then_inc(s["c_rstd"], 1)
                if HSEQ + 1 + b < SEQS:
                    gather(HSEQ + 1 + b)
                pool.wait_ge(s["c_xT"], b + 1)
                for t in range(TPS):
                    if b > 0:
                        pool.wait_ge(s["m_gu"], USEQ * (b - 1) + UNITS * (t + 1))
                    pool.tensor_copy(xc[:, t, :], xn1T[:, t * P:(t + 1) * P]).then_inc(s["c_copy"], 1)

        @block.scalar
        def _(act):
            act.wait_ge(s["dummy_set"], 1)
            nc.scalar.activation(dummy[:, 1:2], dummy[:, 0:1], ACT.Exp).then_inc(s["warm"], 1)

            def xnT_out(h, j):
                act.wait_ge(s["turned"], HSEQ * h + j + 1)
                q = HSEQ * h + j
                nc.scalar.copy(xnT[:, q * SEQ:(q + 1) * SEQ], ps[:, j, :]).then_inc(s["xnT_ready"], 1)

            def lgT_out(h, j):
                act.wait_ge(s["routed"], HSEQ * h + j + 1)
                if HSEQ * h + j >= 2:
                    act.wait_ge(s["lg_turned"], HSEQ * h + j - 1)
                nc.scalar.copy(lgT[:, j % 2, :], ps[0:NR, 4 + j % 2, :]).then_inc(s["lgT_ready"], 1)

            for h in range(HALVES):
                xnT_out(h, 0)
                xnT_out(h, 1)
                lgT_out(h, 0)
                lgT_out(h, 1)
                xnT_out(h, 2)
                xnT_out(h, 3)
                lgT_out(h, 2)
                lgT_out(h, 3)
                act.wait_ge(s["lg_turned"], HSEQ * (h + 1))
                nc.scalar.activation(th_r[:, :, :], ps[:, 6, 0:HT * NR].rearrange("p (t r) -> p t r", r=NR),
                                     ACT.Tanh, scale=0.5).then_inc(s["scored"], 1)
                for j in range(HSEQ):
                    t = HT * h + TPS * j
                    nc.scalar.copy(rows[:, t:t + TPS, 0:P], xnb[:, TPS * j:TPS * (j + 1), :]).then_inc(s["rows_ready"], 1)

            act.wait_ge(s["bias0_ready"], 1)

            def rec_tanh(q, par):
                act.wait_ge(s["rec_mm"], q + 1)
                wait(act, "rec_scan", q - 1)
                nc.scalar.activation(tg[:, par, :], ps[:, 3 * par, :], ACT.Tanh, bias=a0bh[:, 0:1], scale=0.5)
                nc.scalar.activation(tv[:, par, :], ps[:, 3 * par + 1, :], ACT.Tanh, bias=a0b[:, 1:2])
                nc.scalar.activation(td[:, par, :], ps[:, 3 * par + 2, :], ACT.Tanh, bias=a0bh[:, 2:3],
                                     scale=0.5).then_inc(s["rec_act"], 1)

            def rec_out(q, par):
                act.wait_ge(s["rec_turned"], q + 1)
                nc.scalar.copy(seq_of(sT, q), ps[:, 6 + par, :].rearrange("p (t d) -> p t d", d=P)).then_inc(s["rec_out"], 1)

            def rec_pair(i):
                rec_tanh(2 * i, 0)
                if not (isinstance(i, int) and i == 0):
                    rec_out(2 * i - 1, 1)
                rec_tanh(2 * i + 1, 1)
                rec_out(2 * i, 0)

            rec_pair(0)
            with act.Fori(1, SEQS // 2) as i:
                rec_pair(i)
            rec_out(SEQS - 1, 1)

            def sxT_out(n, par):
                act.wait_ge(s["f_turned"], n + 1)
                nc.scalar.copy(sxT[:, par, :], ps[:, 7, 0:P]).then_inc(s["f_xT"], 1)

            def gate_tanh(n, par):
                act.wait_ge(s["f_gate"], n + 1)
                nc.scalar.activation(th0[:, par, :], ps[:, par, :], ACT.Tanh, scale=0.5).then_inc(s["f_th"], 1)

            def h0T_out(n, par):
                act.wait_ge(s["f_hT"], n + 1)
                nc.scalar.copy(h0T[:, par, :], ps[:, 4 + par, :]).then_inc(s["f_hTs"], 1)

            def experts0_pair(i, first=False, last=False):
                for par in range(2):
                    n = 2 * i + par
                    gate_tanh(n, par)
                    if not (last and par == 1):
                        sxT_out(n + 1, 1 - par)
                    if not (first and par == 0):
                        h0T_out(n - 1, 1 - par)

            sxT_out(0, 0)
            experts0_pair(0, first=True)
            with act.Fori(1, SORTED // 2 - 1) as i:
                experts0_pair(i)
            experts0_pair(SORTED // 2 - 1, last=True)
            h0T_out(SORTED - 1, 1)

            def front(k, u):
                if u == 0:
                    act.wait_ge(s["gathered"], 16 * TPS * (k + 1))
                    nc.scalar.activation(thy[:, :].rearrange("p (t d) -> p t d", d=P), seq_of(ya, k),
                                         ACT.Tanh, scale=0.5).then_inc(s["c_th"], 1)
                if u == 10:
                    act.wait_ge(s["c_turned"], k + 1)
                    wait(act, "c_copy", TPS * k)
                    nc.scalar.copy(xn1T[:, :], ps[:, 4, :]).then_inc(s["c_xT"], 1)
                for i, (at_u, name) in enumerate(((13, "c_q"), (14, "c_k"))):
                    if u == at_u:
                        act.wait_ge(s[name], k + 1)
                        nc.scalar.activation(expq[:, i, :], ps[:, 5 + i, :], ACT.Exp, bias=a1b[:, i:i + 1])
                        nc.scalar.activation(linq[:, i, :], ps[:, 5 + i, :], ACT.Identity,
                                             bias=a1b1[:, i:i + 1]).then_inc(s["c_lin"], 1)
                if u == 15:
                    act.wait_ge(s["c_lgm"], k + 1)
                    nc.scalar.activation(e1[:, :, :], lg[:, :, :], ACT.Exp).then_inc(s["c_exp"], 1)

            def unit_tanh(j, u):
                t, p = divmod(u, UNITS)
                n = USEQ * j + u
                if u == 0:
                    act.wait_ge(s["c_scores"], j + 1)
                act.wait_ge(s["m_gu"], n + 1)
                bank = ps[:, u % 2, :]
                if p < PAIRS:
                    for e in range(2):
                        last = nc.scalar.activation(th1[:, u % 2, e * P:(e + 1) * P], bank[:, e * P:(e + 1) * P],
                                                    ACT.Tanh, scale=half_s[:, t, 2 * p + e:2 * p + e + 1])
                else:
                    last = nc.scalar.activation(th1[:, u % 2, 0:P], bank[:, 0:P], ACT.Tanh, scale=0.5)
                last.then_inc(s["m_th"], 1)

            def unit_hT(j, u):
                n = USEQ * j + u
                w = 2 * P if u % UNITS < PAIRS else P
                act.wait_ge(s["m_hT"], n + 1)
                nc.scalar.copy(h1T[:, u % 2, 0:w], ps[:, 2, 0:w]).then_inc(s["m_hTs"], 1)

            def final_tanh(j, t):
                act.wait_ge(s["m_y"], USEQ * j + UNITS * (t + 1))
                nc.scalar.activation(thf[:, t % 2, :], ps[:, 3, 0:P], ACT.Tanh, scale=0.5).then_inc(s["m_thf"], 1)

            def step(k, fronts=True, tiles=True):
                for u in range(USEQ):
                    if tiles:
                        unit_tanh(k - 1, u)
                        if u >= 2:
                            unit_hT(k - 1, u - 2)
                        if u >= UNITS + 2 and (u - 2) % UNITS == 0:
                            final_tanh(k - 1, (u - 2) // UNITS - 1)
                    if fronts:
                        front(k, u)
                if tiles:
                    unit_hT(k - 1, USEQ - 2)
                    unit_hT(k - 1, USEQ - 1)
                    final_tanh(k - 1, TPS - 1)

            act.wait_ge(s["bias1_ready"], 1)
            step(0, tiles=False)
            with act.Fori(1, SEQS) as k:
                step(k)
            step(SEQS, fronts=False)

        @block.tensor
        def _(pe):
            pe.wait_ge(s["consts_in"], 32)

            def turn_xn(h, j):
                pe.wait_ge(s["normed"], HSEQ * h + j + 1)
                for t in range(TPS):
                    last = pe.transpose(ps[:, j, t * P:(t + 1) * P], xnb[:, TPS * j + t, :], ident)
                last.then_inc(s["turned"], 1)

            def route(h, j):
                q = HSEQ * h + j
                pe.wait_ge(s["xnT_ready"], q + 1)
                if q >= 2:
                    pe.wait_ge(s["lgT_ready"], q - 1)
                pe.matmul(ps[0:NR, 4 + j % 2, :], r0[:, :], xnT[:, q * SEQ:(q + 1) * SEQ],
                          start=True, stop=True).then_inc(s["routed"], 1)

            def turn_logits(h, j):
                pe.wait_ge(s["lgT_ready"], HSEQ * h + j + 1)
                if h > 0 and j == 0:
                    pe.wait_ge(s["scored"], h)
                for t in range(TPS):
                    c = (TPS * j + t) * NR
                    last = pe.transpose(ps[:, 6, c:c + NR], lgT[:, j % 2, t * P:(t + 1) * P], ident[0:NR, 0:NR])
                last.then_inc(s["lg_turned"], 1)

            for h in range(HALVES):
                turn_xn(h, 0)
                turn_xn(h, 1)
                route(h, 0)
                route(h, 1)
                turn_xn(h, 2)
                turn_xn(h, 3)
                turn_logits(h, 0)
                turn_logits(h, 1)
                route(h, 2)
                route(h, 3)
                turn_logits(h, 2)
                turn_logits(h, 3)
                pe.wait_ge(s["counted"], h + 1)
                pe.matmul(ps[:, 7, 0:GROUPS], lower, cum[:, :, HT - 1], start=True, stop=True)
                pe.matmul(ps[:, 7, GROUPS:2 * GROUPS], ones, cum[:, :, HT - 1], start=True, stop=True).then_inc(s["placed"], 1)

            pe.wait_ge(s["attn0_in"], 32)

            def rec_project(q, par):
                wait(pe, "rec_act", q - 1)
                for i in range(3):
                    last = pe.matmul(ps[:, 3 * par + i, :], a0w[:, i * P:(i + 1) * P],
                                     xnT[:, bass.ds(q * SEQ, SEQ)], start=True, stop=True)
                last.then_inc(s["rec_mm"], 1)

            def rec_turn(q, par):
                pe.wait_ge(s["rec_scan"], q + 1)
                for t in range(TPS):
                    last = pe.transpose(ps[:, 6 + par, t * P:(t + 1) * P], scan[:, par, t * P:(t + 1) * P], ident)
                last.then_inc(s["rec_turned"], 1)

            def rec_pair(i):
                rec_project(2 * i, 0)
                if not (isinstance(i, int) and i == 0):
                    rec_turn(2 * i - 1, 1)
                rec_project(2 * i + 1, 1)
                rec_turn(2 * i, 0)

            rec_pair(0)
            with pe.Fori(1, SEQS // 2) as i:
                rec_pair(i)
            rec_turn(SEQS - 1, 1)

            pe.wait_ge(s["rec_out"], SEQS)
            pe.wait_ge(s["attn1_in"], 16 * 4)
            pe.wait_ge(s["bias1_ready"], 1)
            pe.matmul(ps[:, 6, 0:P], a1w[:, 2 * P:3 * P], wo[:, :], start=True, stop=True)
            pe.matmul(ps[:, 6, P:2 * P], bv_cols[:, :], wo[:, :], start=True, stop=True).then_inc(s["fused"], 1)

            pe.wait_ge(s["experts0_in"], 32)
            pe.wait_ge(s["group_ready"], HALVES)
            GU = 2 * EPG * F0
            DN = HC * P

            def turn_rows(n, par):
                pe.wait_ge(loaded[par], 16 * (half_of(n, par) + 1))
                pe.transpose(ps[:, 7, 0:P], srow[:, par, 0:P], ident).then_inc(s["f_turned"], 1)

            def gate(n, par, g):
                pe.wait_ge(s["f_xT"], n + 1)
                pe.matmul(ps[:, par, :], sxT[:, par, :], gu0[:, bass.ds(g * GU, GU // 2)],
                          start=True, stop=True).then_inc(s["f_gate"], 1)

            def up(n, par, g):
                pe.matmul(ps[:, 2 + par, :], sxT[:, par, :], gu0[:, bass.ds(g * GU + GU // 2, GU // 2)],
                          start=True, stop=True).then_inc(s["f_up"], 1)

            def turn_h0(n, par):
                pe.wait_ge(s["f_h"], n + 1)
                for c in range(HC):
                    last = pe.transpose(ps[:, 4 + par, c * P:(c + 1) * P], h0[:, par, c * P:(c + 1) * P], ident)
                last.then_inc(s["f_hT"], 1)

            def down(n, par, g):
                pe.wait_ge(s["f_hTs"], n + 1)
                wait(pe, "f_y", n)
                for c in range(HC):
                    last = pe.matmul(ps[:, 6, 0:P], h0T[:, par, c * P:(c + 1) * P],
                                     dn0[:, bass.ds(g * DN + c * P, P)], start=(c == 0), stop=(c == HC - 1))
                last.then_inc(s["f_down"], 1)

            def group_of(n):
                return pe.value_load(group[0:1, bass.ds(n, 1)])

            def experts0_pair(i, first=False, last=False):
                for par in range(2):
                    n = 2 * i + par
                    g = group_of(n)
                    gate(n, par, g)
                    if not (last and par == 1):
                        turn_rows(n + 1, 1 - par)
                    up(n, par, g)
                    if not (first and par == 0):
                        turn_h0(n - 1, 1 - par)
                        down(n - 1, 1 - par, group_of(n - 1))

            turn_rows(0, 0)
            pe.wait_ge(s["fused_out"], 1)
            experts0_pair(0, first=True)
            with pe.Fori(1, SORTED // 2 - 1) as i:
                experts0_pair(i)
            experts0_pair(SORTED // 2 - 1, last=True)
            turn_h0(SORTED - 1, 1)
            down(SORTED - 1, 1, group_of(SORTED - 1))

            pe.wait_ge(s["experts1_in"], 16 * 3)
            pe.wait_ge(s["f_y"], SORTED)

            def front(k, u):
                if u == 9:
                    pe.wait_ge(s["c_xn"], k + 1)
                    for t in range(TPS):
                        last = pe.transpose(ps[:, 4, t * P:(t + 1) * P], xn1[:, t, :], ident)
                    last.then_inc(s["c_turned"], 1)
                if u == 11:
                    pe.wait_ge(s["c_xT"], k + 1)
                    wait(pe, "c_s1", k)
                    pe.matmul(ps[:, 5, :], a1w[:, 0:P], xn1T[:, :], start=True, stop=True).then_inc(s["c_q"], 1)
                if u == 12:
                    pe.matmul(ps[:, 6, :], a1w[:, P:2 * P], xn1T[:, :], start=True, stop=True).then_inc(s["c_k"], 1)
                    for t in range(TPS):
                        o = (t % 2) * (P + E1)
                        last = pe.matmul(ps[:, 7 if t < 2 else 4, o:o + P + E1], xn1T[:, t * P:(t + 1) * P], vg_w[:, :],
                                         start=True, stop=True)
                    last.then_inc(s["c_v"], 1)

            def scores(k, sr):
                bank = (5, 6, 7, 4)[sr]
                if sr == 0:
                    pe.wait_ge(s["c_qkT"], 2 * (k + 1))
                    pe.wait_ge(s["c_lg"], k + 1)
                pe.matmul(ps[:, bank, 0:SEQ - sr * P], kT[:, sr * P:(sr + 1) * P], qT[:, sr * P:SEQ],
                          start=True, stop=True).then_inc(s["c_a"], 1)

            def attend(j):
                pe.wait_ge(s["c_at"], TPS * (j + 1))
                for c in range(TPS):
                    o = (c % 2) * (P + 1)
                    for sr in range(c + 1):
                        last = pe.matmul(ps[:, 5 + c // 2, o:o + P + 1], at[:, sr, c * P:(c + 1) * P], vo[:, sr, :],
                                         start=(sr == 0), stop=(sr == c))
                last.then_inc(s["c_num"], 1)

            def unit_gu(j, u):
                t, p = divmod(u, UNITS)
                w = 4 * P if p < PAIRS else 2 * P
                if p == 0:
                    pe.wait_ge(s["c_copy"], TPS * j + t + 1)
                if u >= 2:
                    pe.wait_ge(s["m_h"], USEQ * j + u - 1)
                pe.matmul(ps[:, u % 2, 0:w], xc[:, t, :], w13s[:, 4 * P * p:4 * P * p + w],
                          start=True, stop=True).then_inc(s["m_gu"], 1)

            def unit_turn(j, u):
                n = USEQ * j + u
                pe.wait_ge(s["m_h"], n + 1)
                if u > 0:
                    pe.wait_ge(s["m_hTs"], n)
                for e in range(2 if u % UNITS < PAIRS else 1):
                    last = pe.transpose(ps[:, 2, e * P:(e + 1) * P], h1[:, u % 2, e * P:(e + 1) * P], ident)
                last.then_inc(s["m_hT"], 1)

            def unit_down(j, u):
                t, p = divmod(u, UNITS)
                n = USEQ * j + u
                pe.wait_ge(s["m_hTs"], n + 1)
                if p == 0:
                    pe.wait_ge(s["m_gf"], 1 + TPS * j + t)
                for e in range(2 if p < PAIRS else 1):
                    last = pe.matmul(ps[:, 3, 0:P], h1T[:, u % 2, e * P:(e + 1) * P],
                                     w2s[:, (2 * p + e) * P:(2 * p + e + 1) * P],
                                     start=(p == 0 and e == 0), stop=(p == PAIRS))
                last.then_inc(s["m_y"], 1)

            def step(k, fronts=True, tiles=True):
                for u in range(USEQ):
                    if tiles:
                        unit_gu(k - 1, u)
                        if u == 1:
                            attend(k - 1)
                        if u >= 2:
                            unit_turn(k - 1, u - 2)
                        if u >= 3:
                            unit_down(k - 1, u - 3)
                    if fronts:
                        front(k, u)
                if fronts:
                    scores(k, 0)
                    scores(k, 1)
                if tiles:
                    unit_turn(k - 1, USEQ - 2)
                    unit_down(k - 1, USEQ - 3)
                if fronts:
                    scores(k, 2)
                    scores(k, 3)
                if tiles:
                    unit_turn(k - 1, USEQ - 1)
                    unit_down(k - 1, USEQ - 2)
                    unit_down(k - 1, USEQ - 1)

            step(0, tiles=False)
            with pe.Fori(1, SEQS) as k:
                step(k)
            step(SEQS, fronts=False)

        @block.vector
        def _(dve):
            chain = [0]

            def link(ins):
                chain[0] += 1
                ins.then_inc(s["chain"], 1)
                dve.wait_ge(s["chain"], chain[0])

            nc.vector.memset(dummy[:, :], 0.0).then_inc(s["dummy_set"], 1)
            dve.sem_inc(s["m_gf"], 1)
            for par in range(2):
                dve.sem_inc(y_stored[par], FREE)
                dve.sem_inc(o_stored[par], FREE)

            def stats(h):
                dve.wait_ge(s["x_in"], 16 * HSEQ * (h + 1))
                for i in range(2):
                    r = range(2 * TPS * i, 2 * TPS * (i + 1))
                    for t in r:
                        last = nc.vector.bn_stats(st[:, t, :], xa[:, HT * h + t, :])
                    link(last)
                    for t in r:
                        last = nc.vector.bn_aggr(mv[:, t, :], st[:, t, :])
                    link(last)
                    nc.vector.tensor_scalar(var[:, r.start:r.stop], mv[:, r.start:r.stop, 1], LN_EPS, None,
                                            ALU.add).then_inc(s["vars"], 1)

            def normalise(h):
                if h > 0:
                    dve.wait_ge(s["turned"], HSEQ * h)
                    dve.wait_ge(s["rows_ready"], HSEQ * h)
                for j in range(HSEQ):
                    if j % 2 == 0:
                        dve.wait_ge(s["rstds"], 2 * h + j // 2 + 1)
                    for t in range(TPS * j, TPS * (j + 1)):
                        last = nc.vector.tensor_scalar(xnb[:, t, :], xa[:, HT * h + t, :], mv[:, t, 0:1], rstd[:, t:t + 1],
                                                       ALU.subtract, ALU.mult)
                    last.then_inc(s["normed"], 1)

            def slots(h):
                dve.wait_ge(s["scored"], h + 1)
                link(nc.vector.tensor_scalar(sc_r[:, :, :], th_r[:, :, :], 0.5, 0.5, ALU.mult, ALU.add))
                macro = sc_r[:, :, 0:GROUPS]
                micro = sc_r[:, :, GROUPS:NR].rearrange("p t (g e) -> p t g e", e=EPG)
                to_groups = [P, HT, GROUPS]
                link(nc.vector.tensor_reduce(best[:, :], macro, AX_X, ALU.max))
                link(nc.vector.tensor_tensor(ohg[:, :, :], macro, best[:, :].unsqueeze(2).broadcast_to(to_groups), ALU.is_ge))
                link(nc.vector.tensor_tensor(ohg[:, :, :], ohg[:, :, :],
                                             fall[:, E1 - GROUPS:E1].unsqueeze(1).broadcast_to(to_groups), ALU.mult))
                link(nc.vector.tensor_reduce(best_e[:, :], ohg[:, :, :], AX_X, ALU.max))
                link(nc.vector.tensor_tensor(ohg[:, :, :], ohg[:, :, :],
                                             best_e[:, :].unsqueeze(2).broadcast_to(to_groups), ALU.is_equal))
                if h > 0:
                    dve.wait_ge(s["placed"], h)
                for g in range(GROUPS):
                    last = nc.vector.tensor_tensor_scan(cum[:, g, :], ones[:, 0:HT], ohg[:, :, g], 0.0, ALU.mult, ALU.add)
                last.then_inc(s["counted"], 1)
                link(nc.vector.tensor_tensor(usum[:, :, :], micro[:, :, :, 0], micro[:, :, :, 1], ALU.add))
                link(nc.vector.tensor_scalar(usum[:, :, :], usum[:, :, :], TOPK_EPS, None, ALU.add))
                link(nc.vector.reciprocal(usum[:, :, :], usum[:, :, :]))
                link(nc.vector.tensor_scalar(mfac[:, :], best[:, :], TOPK_EPS, None, ALU.add))
                link(nc.vector.reciprocal(mfac[:, :], mfac[:, :]))
                link(nc.vector.tensor_tensor(mfac[:, :], mfac[:, :], best[:, :], ALU.mult))
                link(nc.vector.tensor_tensor(usum[:, :, :], usum[:, :, :],
                                             mfac[:, :].unsqueeze(2).broadcast_to(to_groups), ALU.mult))
                link(nc.vector.tensor_tensor(usum[:, :, :], usum[:, :, :], ohg[:, :, :], ALU.mult))
                link(nc.vector.tensor_tensor(uw[:, :, :, :], micro,
                                             usum[:, :, :].unsqueeze(3).broadcast_to([P, HT, GROUPS, EPG]), ALU.mult))
                nc.vector.tensor_reduce(rows[:, HT * h:HT * (h + 1), P:ROW], uw[:, :, :, :].rearrange("p t g e -> p t e g"),
                                        AX_X, ALU.add)
                dve.wait_ge(s["placed"], h + 1)
                link(nc.vector.tensor_copy(tot[:, :], ps[:, 7, 0:2 * GROUPS]))
                link(nc.vector.tensor_scalar(ntile[:, :], tot[:, GROUPS:2 * GROUPS], 1.0 / P, (P / 2 - 0.5) / P,
                                             ALU.mult, ALU.add))
                link(nc.vector.tensor_scalar(ntile[:, :], ntile[:, :], MAGIC, MAGIC, ALU.add, ALU.subtract))
                link(nc.vector.tensor_tensor_scan(ends[:, :], ones[:, 0:GROUPS], ntile[:, :], 0.0, ALU.mult, ALU.add))
                link(nc.vector.tensor_tensor(base[:, :], ends[:, :], ntile[:, :], ALU.subtract))
                link(nc.vector.scalar_tensor_tensor(base[:, :], base[:, :], float(P), tot[:, 0:GROUPS], ALU.mult, ALU.add))
                link(nc.vector.tensor_scalar(base[:, :], base[:, :], float(h * FT * P - 1), None, ALU.add))
                link(nc.vector.tensor_tensor(where[:, :, :], cum[:, :, :],
                                             base[:, :].unsqueeze(2).broadcast_to([P, GROUPS, HT]), ALU.add))
                link(nc.vector.tensor_tensor(where[:, :, :], where[:, :, :], ohg[:, :, :].rearrange("p t g -> p g t"), ALU.mult))
                link(nc.vector.tensor_reduce(slot_f[:, :], where[:, :, :].rearrange("p g t -> p t g"), AX_X, ALU.add))
                nc.vector.tensor_copy(slot[:, HT * h:HT * (h + 1)], slot_f[:, :]).then_inc(s["slots_ready"], 1)
                link(nc.vector.tensor_tensor(past[0:1, :, :],
                                             cst[0:1, C_TILE:C_TILE + FT].unsqueeze(2).broadcast_to([1, FT, GROUPS - 1]),
                                             ends[0:1, 0:GROUPS - 1].unsqueeze(1).broadcast_to([1, FT, GROUPS - 1]), ALU.is_ge))
                link(nc.vector.tensor_reduce(group_f[:, :], past[0:1, :, :], AX_X, ALU.add))
                nc.vector.tensor_copy(group[:, FT * h:FT * (h + 1)], group_f[:, :]).then_inc(s["group_ready"], 1)

            stats(0)
            normalise(0)
            stats(1)
            dve.wait_ge(s["consts_in"], 32)
            slots(0)
            normalise(1)
            dve.wait_ge(s["attn0_in"], 32)
            nc.vector.tensor_scalar(a0bh[:, :], a0b[:, :], 0.5, None, ALU.mult).then_inc(s["bias0_ready"], 1)
            dve.wait_ge(s["attn1_in"], 16 * 4)
            nc.vector.tensor_scalar(a1b1[:, :], a1b[:, 0:2], 1.0, None, ALU.add)
            nc.vector.tensor_scalar(bv_cols[:, :], ones, a1b[:, 2:3], None, ALU.mult).then_inc(s["bias1_ready"], 1)
            slots(1)

            def rec_scan(q, par):
                dve.wait_ge(s["rec_act"], q + 1)
                nc.vector.tensor_scalar(td[:, par, :], td[:, par, :], 0.499, 0.5, ALU.mult, ALU.add).then_inc(s["rec_x"], 1)
                nc.vector.scalar_tensor_tensor(tg[:, par, :], tg[:, par, :], 1.0, tv[:, par, :],
                                               ALU.add, ALU.mult).then_inc(s["rec_x"], 1)
                dve.wait_ge(s["rec_x"], 2 * q + 2)
                wait(dve, "rec_turned", q - 1)
                nc.vector.tensor_tensor_scan(scan[:, par, :], td[:, par, :], tg[:, par, :], 0.0,
                                             ALU.mult, ALU.add).then_inc(s["rec_scan"], 1)

            def rec_pair(i):
                rec_scan(2 * i, 0)
                rec_scan(2 * i + 1, 1)

            rec_pair(0)
            with dve.Fori(1, SEQS // 2) as i:
                rec_pair(i)

            dve.wait_ge(s["fused"], 1)
            nc.vector.tensor_copy(vg_w[:, 0:P], ps[:, 6, 0:P])
            nc.vector.tensor_copy(bv_wo[:, :], ps[:, 6, P:2 * P]).then_inc(s["fused_out"], 1)

            def weights(n, par):
                dve.wait_ge(loaded[par], 16 * (half_of(n, par) + 1))
                wait(dve, "f_h", n - 1)
                nc.vector.tensor_scalar(sw[:, par, :], srow[:, par, P:ROW], 0.5, None, ALU.mult).then_inc(s["f_w"], 1)

            def hidden(n, par):
                dve.wait_ge(s["f_th"], n + 1)
                wait(dve, "f_hT", n - 1)
                nc.vector.scalar_tensor_tensor(h0[:, par, :], th0[:, par, :], 1.0, ps[:, par, :],
                                               ALU.add, ALU.mult).then_inc(s["f_a"], 1)
                dve.wait_ge(s["f_a"], n + 1)
                dve.wait_ge(s["f_up"], n + 1)
                for e in range(EPG):
                    c = slice(e * F0, (e + 1) * F0)
                    last = nc.vector.scalar_tensor_tensor(h0[:, par, c], h0[:, par, c], sw[:, par, e:e + 1],
                                                          ps[:, 2 + par, c], ALU.mult, ALU.mult)
                last.then_inc(s["f_h"], 1)

            def result(n, par):
                dve.wait_ge(s["f_down"], n + 1)
                dve.wait_ge(y_stored[par], FREE + 16 * half_of(n, par))
                nc.vector.tensor_copy(y0[:, par, :], ps[:, 6, 0:P]).then_inc(s["f_y"], 1)

            def experts0_pair(i, first=False, last=False):
                for par in range(2):
                    n = 2 * i + par
                    if not (last and par == 1):
                        weights(n + 1, 1 - par)
                    hidden(n, par)
                    if not (first and par == 0):
                        result(n - 1, 1 - par)

            weights(0, 0)
            dve.wait_ge(s["f_w"], 1)
            experts0_pair(0, first=True)
            with dve.Fori(1, SORTED // 2 - 1) as i:
                experts0_pair(i)
            experts0_pair(SORTED // 2 - 1, last=True)
            result(SORTED - 1, 1)

            R_AT = (1, 1, 1, 0, 1, 1, 0, 0, 0, 0, 0, 0, 0, 1, 0, 0, 3, 5, 6, 2)
            R_STEPS = sum(R_AT)

            def front(k, u):
                n = [R_STEPS * k + sum(R_AT[:u])]

                def then(ins):
                    n[0] = n[0] + 1
                    ins.then_inc(s["c_chain"], 1)
                    dve.wait_ge(s["c_chain"], n[0])

                by_expert = [P, TPS, E1]
                g3 = gy[:, :].rearrange("p (t d) -> p t d", d=P)
                if u == 0:
                    dve.wait_ge(s["c_th"], k + 1)
                    then(nc.vector.scalar_tensor_tensor(g3, thy[:, :].rearrange("p (t d) -> p t d", d=P), 1.0,
                                                        seq_of(ya, k), ALU.add, ALU.mult))
                if u == 1:
                    then(nc.vector.tensor_tensor(g3, g3, seq_of(sT, k), ALU.mult))
                if u == 2:
                    then(nc.vector.scalar_tensor_tensor(seq_of(xa, k), g3, 0.25, seq_of(xa, k), ALU.mult, ALU.add))
                if u == 4:
                    for t in range(TPS):
                        last = nc.vector.bn_stats(st1[:, t, :], xa[:, bass.ds(k * TPS + t, 1), :].rearrange("p o d -> p (o d)"))
                    then(last)
                if u == 5:
                    for t in range(TPS):
                        last = nc.vector.bn_aggr(mv1[:, t, :], st1[:, t, :])
                    then(last)
                    nc.vector.tensor_scalar(var1[:, :], mv1[:, :, 1], LN_EPS, None, ALU.add).then_inc(s["c_var"], 1)
                if u == 8:
                    dve.wait_ge(s["c_rstd"], k + 1)
                    for t in range(TPS):
                        last = nc.vector.tensor_scalar(xn1[:, t, :], xa[:, bass.ds(k * TPS + t, 1), :].rearrange("p o d -> p (o d)"),
                                                       mv1[:, t, 0:1], rstd1[:, t:t + 1], ALU.subtract, ALU.mult)
                    last.then_inc(s["c_xn"], 1)
                if u == 13:
                    dve.wait_ge(s["c_v"], k + 1)
                    for i, bank in enumerate((7, 4)):
                        two = ps[:, bank, 0:2 * (P + E1)].rearrange("p (t c) -> p t c", c=P + E1)
                        nc.vector.tensor_tensor(vo[:, 2 * i:2 * i + 2, 0:P], two[:, :, 0:P],
                                                bv_wo[:, :].unsqueeze(1).broadcast_to([P, 2, P]), ALU.add)
                        last = nc.vector.tensor_copy(lg[:, 2 * i:2 * i + 2, :], two[:, :, P:P + E1])
                    last.then_inc(s["c_lg"], 1)
                    dve.wait_ge(s["c_lg"], k + 1)
                    then(nc.vector.tensor_reduce(rm[:, :], lg[:, :, :], AX_X, ALU.max))
                    nc.vector.tensor_tensor(lg[:, :, :], lg[:, :, :], rm[:, :].unsqueeze(2).broadcast_to(by_expert),
                                            ALU.subtract).then_inc(s["c_lgm"], 1)
                for i, at_u in enumerate((14, 15)):
                    if u == at_u:
                        dve.wait_ge(s["c_lin"], 2 * k + i + 1)
                        nc.vector.scalar_tensor_tensor((qT, kT)[i][:, :], expq[:, i, :], 1.0, linq[:, i, :],
                                                       ALU.min, ALU.max).then_inc(s["c_qkT"], 1)
                if u == 16:
                    dve.wait_ge(s["c_exp"], k + 1)
                    then(nc.vector.tensor_reduce(rs[:, :], e1[:, :, :], AX_X, ALU.add))
                    then(nc.vector.reciprocal(rs[:, :], rs[:, :]))
                    then(nc.vector.tensor_tensor(pr[:, :, :], e1[:, :, :], rs[:, :].unsqueeze(2).broadcast_to(by_expert), ALU.mult))
                for at_u, src, oh in ((17, pr, oh1), (18, rq, oh2)):
                    if u == at_u:
                        if oh is oh2:
                            then(nc.vector.scalar_tensor_tensor(rq[:, :, :], oh1[:, :, :], -2.0, pr[:, :, :], ALU.mult, ALU.add))
                        then(nc.vector.tensor_reduce(rm[:, :], src[:, :, :], AX_X, ALU.max))
                        then(nc.vector.tensor_tensor(oh[:, :, :], src[:, :, :], rm[:, :].unsqueeze(2).broadcast_to(by_expert), ALU.is_ge))
                        then(nc.vector.tensor_tensor(oh[:, :, :], oh[:, :, :], fall.unsqueeze(1).broadcast_to(by_expert), ALU.mult))
                        then(nc.vector.tensor_reduce(rs[:, :], oh[:, :, :], AX_X, ALU.max))
                        then(nc.vector.tensor_tensor(oh[:, :, :], oh[:, :, :], rs[:, :].unsqueeze(2).broadcast_to(by_expert), ALU.is_equal))
                if u == 19:
                    then(nc.vector.tensor_tensor(oh1[:, :, :], oh1[:, :, :], oh2[:, :, :], ALU.add))
                    then(nc.vector.tensor_tensor(pr[:, :, :], pr[:, :, :], oh1[:, :, :], ALU.mult))
                assert not isinstance(k, int) or n[0] == R_STEPS * k + sum(R_AT[:u + 1]), (u, n)

            def scaled_scores(k):
                nc.vector.tensor_scalar(half_s[:, :, :], pr[:, :, :], 0.5, None, ALU.mult)
                nc.vector.scalar_tensor_tensor(half_s2[:, :, :], pr[:, :, :], 0.5, pr[:, :, :],
                                               ALU.mult, ALU.mult).then_inc(s["c_scores"], 1)

            def masked(k, sr):
                dve.wait_ge(s["c_a"], TPS * k + sr + 1)
                w = SEQ - sr * P
                nc.vector.tensor_tensor(at[:, sr, sr * P:SEQ], ps[:, (5, 6, 7, 4)[sr], 0:w], cst[:, C_CAUSAL:C_CAUSAL + w],
                                        ALU.mult).then_inc(s["c_at"], 1)

            def attention(j):
                dve.wait_ge(s["c_num"], j + 1)
                for i in range(2):
                    nc.vector.tensor_scalar(den[:, 2 * i:2 * i + 2],
                                            ps[:, 5 + i, 0:2 * (P + 1)].rearrange("p (t c) -> p t c", c=P + 1)[:, :, P],
                                            ATT_EPS, None, ALU.add).then_inc(s["c_den"], 1)
                dve.wait_ge(s["c_den"], 3 * j + 2)
                nc.vector.reciprocal(den[:, :], den[:, :]).then_inc(s["c_den"], 1)
                dve.wait_ge(s["c_den"], 3 * j + 3)
                for c in range(TPS):
                    o = (c % 2) * (P + 1)
                    last = nc.vector.scalar_tensor_tensor(s1[:, c, :], ps[:, 5 + c // 2, o:o + P], den[:, c:c + 1], bo[:, :],
                                                          ALU.mult, ALU.add)
                last.then_inc(s["c_s1"], 1)

            def unit(j, u):
                t, p = divmod(u, UNITS)
                n = USEQ * j + u
                w = 2 * P if p < PAIRS else P
                bank = ps[:, u % 2, :]
                dve.wait_ge(s["m_th"], n + 1)
                nc.vector.scalar_tensor_tensor(a1[:, u % 2, 0:w], th1[:, u % 2, 0:w], 1.0, bank[:, 0:w],
                                               ALU.add, ALU.mult).then_inc(s["m_a"], 1)
                dve.wait_ge(s["m_a"], n + 1)
                if u >= 2:
                    dve.wait_ge(s["m_hT"], n - 1)
                for e in range(w // P):
                    c = slice(e * P, (e + 1) * P)
                    last = nc.vector.scalar_tensor_tensor(
                        h1[:, u % 2, c], a1[:, u % 2, c], half_s2[:, t, 2 * p + e:2 * p + e + 1] if p < PAIRS else 0.5,
                        bank[:, w + e * P:w + (e + 1) * P], ALU.mult, ALU.mult)
                last.then_inc(s["m_h"], 1)

            def final(j, t):
                par = t % 2
                m = TPS * j + t
                dve.wait_ge(s["m_thf"], m + 1)
                nc.vector.scalar_tensor_tensor(gf[:, par, :], thf[:, par, :], 1.0, ps[:, 3, 0:P],
                                               ALU.add, ALU.mult).then_inc(s["m_gf"], 1)
                dve.wait_ge(s["m_gf"], 1 + m + 1)
                nc.vector.tensor_tensor(of[:, par, :], gf[:, par, :], s1[:, t, :], ALU.mult).then_inc(s["m_of"], 1)
                dve.wait_ge(s["m_of"], m + 1)
                dve.wait_ge(o_stored[par], FREE + 16 * (2 * j + t // 2))
                nc.vector.scalar_tensor_tensor(xo[:, par, :], of[:, par, :], 0.5,
                                               xa[:, bass.ds(m, 1), :].rearrange("p o d -> p (o d)"),
                                               ALU.mult, ALU.add).then_inc(s["m_xo"], 1)

            def step(k, fronts=True, tiles=True):
                for u in range(USEQ):
                    if tiles:
                        unit(k - 1, u)
                        if u == 3:
                            attention(k - 1)
                        if u >= UNITS + 2 and (u - 2) % UNITS == 0:
                            final(k - 1, (u - 2) // UNITS - 1)
                    if fronts:
                        front(k, u)
                if fronts:
                    scaled_scores(k)
                    for sr in range(TPS):
                        masked(k, sr)
                if tiles:
                    final(k - 1, TPS - 1)

            step(0, tiles=False)
            with dve.Fori(1, SEQS) as k:
                step(k)
            step(SEQS, fronts=False)


def kernel(**inputs):
    import numpy as np
    import concourse.bacc as bacc
    from concourse import mybir as mb
    from concourse.bass_utils import run_bass_kernel_spmd

    f = {k: np.asarray(v) for k, v in inputs.items()}
    cat = np.concatenate

    consts = np.zeros((P, CONSTS), np.float32)
    consts[:, C_ID:C_ID + P] = np.eye(P)
    consts[:, C_LOWER:C_LOWER + P] = np.triu(np.ones((P, P)), 1)
    consts[:, C_CAUSAL:C_CAUSAL + P] = np.triu(np.ones((P, P)))
    consts[:, C_ONES:C_FALL] = 1.0
    consts[:, C_FALL:C_FALL + E1] = np.arange(E1, 0, -1)
    consts[:, C_TILE:C_TILE + FT] = np.arange(FT)

    def columns(*names):
        return np.stack([f[n] for n in names], axis=1)

    ge = lambda w: w.reshape(GROUPS, EPG, P, F0).transpose(2, 0, 1, 3).reshape(P, GROUPS, EPG * F0)
    gate_up0 = cat([ge(f["L0_ffn_gate_w"]), ge(f["L0_ffn_up_w"])], axis=2).reshape(P, -1)
    down0 = f["L0_ffn_down_w"].reshape(GROUPS, HC, P, P).transpose(2, 0, 1, 3).reshape(P, -1)
    micro = f["L0_ffn_micro_w"].transpose(1, 0, 2).reshape(P, -1)
    pairs = lambda w: w.reshape(PAIRS, 2, P, P).transpose(2, 0, 1, 3).reshape(P, PAIRS, 2 * P)
    w13 = cat([cat([pairs(f["L1_ffn_w1"]), pairs(f["L1_ffn_w3"])], axis=2).reshape(P, -1),
               f["L1_ffn_w1s"][0], f["L1_ffn_w3s"][0], f["L1_ffn_gate_w"].T], axis=1)
    w2 = cat([f["L1_ffn_w2"].transpose(1, 0, 2).reshape(P, -1), f["L1_ffn_w2s"][0]], axis=1)
    arrays = {
        "x": f["L0_attn_x"],
        "consts": consts,
        "router0": cat([f["L0_ffn_macro_w"], micro], axis=1),
        "attn0_w": cat([f["L0_attn_Wg"].T, f["L0_attn_Wv"].T, f["L0_attn_Wd"].T], axis=1),
        "attn0_b": columns("L0_attn_bg", "L0_attn_bv", "L0_attn_bd"),
        "gate_up0": gate_up0,
        "down0": down0,
        "attn1_w": cat([f["L1_attn_Wq"].T, f["L1_attn_Wk"].T, f["L1_attn_Wv"]], axis=1),
        "attn1_b": columns("L1_attn_bq", "L1_attn_bk", "L1_attn_bv"),
        "wo1": f["L1_attn_Wo"].T,
        "bo1": np.tile(f["L1_attn_bo"], (P, 1)),
        "w13": w13,
        "w2": w2,
    }
    nc = bacc.Bacc("TRN2", target_bir_lowering=False, num_devices=1)
    named, args = {}, []
    for name, a in arrays.items():
        a = np.ascontiguousarray(a)
        named[f"in_{name}"] = a
        args.append(nc.dram_tensor(f"in_{name}", a.shape, mb.dt.from_np(a.dtype), kind="ExternalInput").ap())
    args.append(nc.dram_tensor("out_x", arrays["x"].shape, mb.dt.from_np(arrays["x"].dtype), kind="ExternalOutput").ap())
    gated_recurrent_moe_two_layers(nc, *args)
    r = run_bass_kernel_spmd(nc, [named], core_ids=[0])
    return r.results[0]["out_x"]
```

```python
from contextlib import ExitStack

import concourse.bass as bass
from concourse import mybir

ALU = mybir.AluOpType
ACT = mybir.ActivationFunctionType
AX_X = mybir.AxisListType.X
F32 = mybir.dt.float32
I32 = mybir.dt.int32
U32 = mybir.dt.uint32

P = 128
SEQS = 8
TPS = 4
SEQ = TPS * P
TILES = SEQS * TPS
HALVES = 2
HT = TILES // HALVES
HSEQ = SEQS // HALVES
GROUPS = 4
EPG = 2
F0 = 256
FT = HT + GROUPS - 1
SORTED = HALVES * FT
ROW = P + EPG
HC = EPG * F0 // P
E1 = 8
PAIRS = E1 // 2
UNITS = PAIRS + 1
USEQ = UNITS * TPS
GU0 = EPG * F0
W0 = 2 * GU0 + HC * P
NR = GROUPS + GROUPS * EPG
LN_EPS = 1e-5
TOPK_EPS = 1e-9
ATT_EPS = 1e-6
MAGIC = float(1 << 23)

C_ID, C_LOWER, C_CAUSAL, C_ONES = (i * P for i in range(4))
C_FALL = C_CAUSAL + SEQ
C_TILE = C_FALL + E1
CONSTS = C_TILE + FT


def gated_recurrent_moe_two_layers(
    nc, x, consts, router0, attn0_w, attn0_b, experts0,
    attn1_w, attn1_b, wo1, bo1, w13, w2, out,
):
    ctx = ExitStack()
    with ctx:
        def sb(name, shape, dt=F32):
            return ctx.enter_context(nc.sbuf_tensor(name, shape, dt))

        def sem(name):
            return ctx.enter_context(nc.semaphore(name))

        sorted_rows = nc.dram_tensor("sorted_rows", [SORTED * P, ROW], F32, kind="Internal").ap()
        sorted_y = nc.dram_tensor("sorted_y", [SORTED * P, P], F32, kind="Internal").ap()
        x_t = x.rearrange("b (t p) d -> b p t d", p=P)
        out_t = out.rearrange("b (t p) d -> (b t) p d", p=P)
        rows_t = sorted_rows.rearrange("(n p) c -> p n c", p=P)
        y_t = sorted_y.rearrange("(n p) c -> p n c", p=P)

        ps = ctx.enter_context(nc.psum_tensor("ps", [P, 8, 512], F32))

        cst = sb("cst", [P, CONSTS])
        ident = cst[:, C_ID:C_ID + P]
        lower = cst[:, C_LOWER:C_LOWER + P]
        ones = cst[:, C_ONES:C_ONES + P]
        fall = cst[:, C_FALL:C_FALL + E1]
        r0 = sb("r0", [P, NR])
        a0w = sb("a0w", [P, 3 * P])
        a0b = sb("a0b", [P, 3])
        a0bh = sb("a0bh", [P, 3])
        w0s = sb("w0s", [P, GROUPS * W0])
        a1w = sb("a1w", [P, 3 * P])
        a1b = sb("a1b", [P, 3])
        a1b1 = sb("a1b1", [P, 2])
        wo = sb("wo", [P, P])
        bo = sb("bo", [P, P])
        w13s = sb("w13s", [P, (2 * E1 + 2) * P])
        w2s = sb("w2s", [P, (E1 + 1) * P])
        vg_w = sb("vg_w", [P, P + E1])
        bv_wo = sb("bv_wo", [P, P])
        bv_cols = sb("bv_cols", [P, P])
        minus_half = sb("minus_half", [P, 2 * TPS])
        zero_rows = sb("zero_rows", [P, 2 * ROW])
        warm = sb("warm", [P, 1])

        xa = sb("xa", [P, TILES, P])
        xnT = sb("xnT", [P, SEQS * SEQ])
        sorted_sb = sb("sorted_sb", [P, FT + TILES, ROW])
        rows = sorted_sb[:, FT:FT + TILES, :]
        slot = sb("slot", [P, TILES], U32)
        group = sb("group", [1, SORTED], I32)
        sT = sb("sT", [P, TILES, P])
        ya = xnT[:, :].rearrange("p (t d) -> p t d", d=P)

        st = sb("st", [P, HT, 6])
        mv = sb("mv", [P, HT, 2])
        var = sb("var", [P, HT])
        rstd = sb("rstd", [P, HT])
        xnb = sb("xnb", [P, HT, P])
        lgT = sb("lgT", [NR, 2, SEQ])
        th_r = sb("th_r", [P, HT, NR])
        sc_r = sb("sc_r", [P, HT, NR])
        best = sb("best", [P, HT])
        best_e = sb("best_e", [P, HT])
        mfac = sb("mfac", [P, HT])
        ohg = sb("ohg", [P, HT, GROUPS])
        cum = sb("cum", [P, GROUPS, HT])
        cnt = sb("cnt", [P, GROUPS])
        tot = sb("tot", [P, 2 * GROUPS])
        ntile = sb("ntile", [P, GROUPS])
        ends = sb("ends", [P, GROUPS])
        base = sb("base", [P, GROUPS])
        where = sb("where", [P, GROUPS, HT])
        slot_f = sb("slot_f", [P, HT])
        group_f = sb("group_f", [1, FT])
        past = sb("past", [P, FT, GROUPS - 1])
        usum = sb("usum", [P, HT, GROUPS])
        uw = sb("uw", [P, HT, GROUPS, EPG])

        tg = sb("tg", [P, 2, SEQ])
        tv = sb("tv", [P, 2, SEQ])
        td = sb("td", [P, 2, SEQ])
        scan = sb("scan", [P, 2, SEQ])

        srow = sb("srow", [P, 2, ROW])
        sw = sb("sw", [P, 2, EPG])
        sxT = sb("sxT", [P, 2, P])
        th0 = sb("th0", [P, 2, 512])
        dummy = sb("first_act", [P, 2])
        h0 = sb("h0", [P, 2, 512])
        h0T = sb("h0T", [P, 2, 512])

        thy = sb("thy", [P, SEQ])
        gy = sb("gy", [P, SEQ])
        st1 = sb("st1", [P, TPS, 6])
        mv1 = sb("mv1", [P, TPS, 2])
        var1 = sb("var1", [P, TPS])
        rstd1 = sb("rstd1", [P, TPS])
        xn1 = sb("xn1", [P, TPS, P])
        xn1T = sb("xn1T", [P, SEQ])
        xc = sb("xc", [P, TPS, P])
        expq, linq = tg, tv
        qT = sb("qT", [P, SEQ])
        kT = sb("kT", [P, SEQ])
        vo = sb("vo", [P, TPS, P + 1])
        at = xnb[:, :, :].rearrange("p (s t) d -> p s (t d)", s=TPS)
        lg = sb("lg", [P, TPS, E1])
        e1 = sb("e1", [P, TPS, E1])
        pr = sb("pr", [P, TPS, E1])
        rq = sb("rq", [P, TPS, E1])
        oh1 = sb("oh1", [P, TPS, E1])
        oh2 = sb("oh2", [P, TPS, E1])
        rm = sb("rm", [P, TPS])
        rs = sb("rs", [P, TPS])
        half_s = sb("half_s", [P, TPS, E1])
        half_s2 = sb("half_s2", [P, TPS, E1])
        den = sb("den", [P, TPS])
        s1 = sb("s1", [P, TPS, P])
        th1 = sb("th1", [P, 2, 2 * P])
        a1 = sb("a1", [P, 2, 2 * P])
        h1 = sb("h1", [P, 2, 2 * P])
        h1T = sb("h1T", [P, 2, 2 * P])
        thf = sb("thf", [P, 2, P])
        gf = sb("gf", [P, 2, P])
        of = sb("of", [P, 2, P])
        xo = sb("xo", [P, 2, P])

        names = """dummy_set warm x_in consts_in attn0_in attn1_in experts0_in experts1_in zeroed zero_tile pool_const
            chain vars rstds normed turned xnT_ready routed lgT_ready lg_turned scored rows_ready
            counted placed slots_ready group_ready bias0_ready bias1_ready
            rec_mm rec_act rec_x rec_scan rec_turned rec_out fused fused_out
            f_row f_turned f_w f_xT f_gate f_up f_th f_a f_h f_hT f_hTs f_down f_y gathered
            c_chain c_th c_var c_rstd c_xn c_turned c_xT c_copy c_q c_k c_lin c_qkT
            c_v c_lg c_lgm c_exp c_scores c_a c_at c_num c_den c_s1
            m_gu m_th m_a m_h m_hT m_hTs m_y m_thf m_gf m_of m_xo""".split()
        s = {n: sem(n) for n in names}
        sorted_in = [sem(f"sorted_in{h}") for h in range(HALVES)]
        y_stored = [sem(f"y_stored{h}") for h in range(HALVES)]
        o_stored = [sem(f"o_stored{i}") for i in range(2)]

        def wait(eng, name, value):
            if not (isinstance(value, int) and value <= 0):
                eng.wait_ge(s[name] if isinstance(name, str) else name, value)

        FREE = 16
        scattered = [sem(f"scattered{h}") for h in range(HALVES)]

        def tile_of(tiles, n):
            return tiles[bass.ds(n, 1)].rearrange("o p c -> (o p) c")

        def seq_of(tiles, q):
            return tiles[:, bass.ds(q * TPS, TPS), :]

        def tile_at(tiles, n):
            return tiles[:, bass.ds(n, 1), :].rearrange("p o c -> p (o c)")

        block = ctx.enter_context(nc.Block())

        @block.sync
        def _(sp):
            for q in range(HSEQ):
                sp.dma_start(xa[:, TPS * q:TPS * (q + 1), :], x_t[q]).then_inc(s["x_in"], 16)
            sp.dma_start(cst[:, :], consts).then_inc(s["consts_in"], 16)
            sp.dma_start(r0[:, :], router0).then_inc(s["consts_in"], 16)
            sp.wait_ge(s["x_in"], 16 * HSEQ)
            for q in range(HSEQ, SEQS):
                sp.dma_start(xa[:, TPS * q:TPS * (q + 1), :], x_t[q]).then_inc(s["x_in"], 16)
            sp.dma_start(a0w[:, :], attn0_w).then_inc(s["attn0_in"], 16)
            sp.dma_start(a0b[:, :], attn0_b).then_inc(s["attn0_in"], 16)
            sp.wait_ge(s["zero_tile"], 1)
            sp.dma_start(sorted_rows.rearrange("(p n r) c -> p n (r c)", p=P, r=2),
                         zero_rows[:, :].unsqueeze(1).broadcast_to([P, SORTED // 2, 2 * ROW])).then_inc(s["zeroed"], 16)
            for to, src in ((a1w, attn1_w), (a1b, attn1_b), (wo, wo1), (bo, bo1)):
                sp.dma_start(to[:, :], src).then_inc(s["attn1_in"], 16)
            sp.dma_start(w0s[:, :], experts0).then_inc(s["experts0_in"], 16)
            sp.dma_start(vg_w[:, P:P + E1], w13[:, (2 * E1 + 2) * P:]).then_inc(s["experts1_in"], 16)
            sp.dma_start(w13s[:, :], w13[:, 0:(2 * E1 + 2) * P]).then_inc(s["experts1_in"], 16)
            sp.dma_start(w2s[:, :], w2).then_inc(s["experts1_in"], 16)

            for h in range(HALVES):
                sp.wait_ge(scattered[h], 16 * HT)
                n = slice(FT * h, FT * (h + 1))
                sp.dma_start(sorted_sb[:, n, :], rows_t[:, n, :]).then_inc(sorted_in[h], 16)
            for h in range(HALVES):
                sp.wait_ge(s["f_y"], FT * (h + 1))
                n = slice(FT * h, FT * (h + 1))
                sp.dma_start(y_t[:, n, :], sorted_sb[:, n, 0:P]).then_inc(y_stored[h], 16)

            with sp.Fori(0, SEQS) as b:
                for t in range(TPS):
                    sp.wait_ge(s["m_xo"], b * TPS + t + 1)
                    sp.dma_start(tile_of(out_t, b * TPS + t), xo[:, t % 2, :]).then_inc(o_stored[t % 2], 16)
            for par in range(2):
                sp.wait_ge(o_stored[par], FREE + 16 * TILES // 2)
            for h in range(HALVES):
                sp.wait_ge(y_stored[h], 16)

        @block.gpsimd
        def _(pool):
            pool.memset(minus_half[:, :], -0.5).then_inc(s["pool_const"], 1)
            pool.memset(zero_rows[:, :], 0.0).then_inc(s["zero_tile"], 1)
            pool.memset(vo[:, :, P:P + 1], 1.0).then_inc(s["pool_const"], 1)
            pool.wait_ge(s["pool_const"], 2)

            for i in range(2 * HALVES):
                pool.wait_ge(s["vars"], i + 1)
                if i >= 2:
                    pool.wait_ge(s["normed"], 2 * (i - 1))
                part = slice((i % 2) * 2 * TPS, (i % 2 + 1) * 2 * TPS)
                pool.tensor_tensor(rstd[:, part], var[:, part], minus_half[:, :], ALU.pow).then_inc(s["rstds"], 1)

            pool.wait_ge(s["zeroed"], 16)
            for h in range(HALVES):
                pool.wait_ge(s["slots_ready"], h + 1)
                pool.wait_ge(s["rows_ready"], HSEQ * (h + 1))
                for t in range(HT * h, HT * (h + 1)):
                    pool.indirect_dma_start(
                        sorted_rows, bass.IndirectOffsetOnAxis(ap=slot[:, t:t + 1], axis=0),
                        rows[:, t, :], None).then_inc(scattered[h], 16)

            def gather(b):
                if b % HSEQ == 0:
                    pool.wait_ge(y_stored[b // HSEQ], 16)
                if b > 0:
                    pool.wait_ge(s["gathered"], 16 * TPS * b)
                for t in range(TPS * b, TPS * (b + 1)):
                    pool.indirect_dma_start(
                        ya[:, t, :], None, sorted_y[0:FT * P * (b // HSEQ + 1)],
                        bass.IndirectOffsetOnAxis(ap=slot[:, t:t + 1], axis=0)).then_inc(s["gathered"], 16)

            def row_at_hand(n, par):
                wait(pool, "f_turned", n - 1)
                wait(pool, "f_w", n - 1)
                pool.tensor_copy(srow[:, par, :], tile_at(sorted_sb, n)).then_inc(s["f_row"], 1)

            def rows_at_hand(i):
                for par in range(2):
                    row_at_hand(2 * i + par, par)

            mid = FT // 2
            pool.wait_ge(sorted_in[0], 16)
            rows_at_hand(0)
            with pool.Fori(1, mid) as i:
                rows_at_hand(i)
            pool.wait_ge(sorted_in[1], 16)
            late = SORTED // 2 - HSEQ
            with pool.Fori(mid, late) as i:
                rows_at_hand(i)
            for b in range(HSEQ):
                rows_at_hand(late + b)
                gather(b)
            gather(HSEQ)
            for b in range(SEQS):
                pool.wait_ge(s["c_var"], b + 1)
                pool.tensor_tensor(rstd1[:, :], var1[:, :], minus_half[:, 0:TPS], ALU.pow).then_inc(s["c_rstd"], 1)
                if HSEQ + 1 + b < SEQS:
                    gather(HSEQ + 1 + b)
                pool.wait_ge(s["c_xT"], b + 1)
                for t in range(TPS):
                    if b > 0:
                        pool.wait_ge(s["m_gu"], USEQ * (b - 1) + UNITS * (t + 1))
                    pool.tensor_copy(xc[:, t, :], xn1T[:, t * P:(t + 1) * P]).then_inc(s["c_copy"], 1)

        @block.scalar
        def _(act):
            act.wait_ge(s["dummy_set"], 1)
            nc.scalar.activation(dummy[:, 1:2], dummy[:, 0:1], ACT.Exp).then_inc(s["warm"], 1)

            def xnT_out(h, j):
                act.wait_ge(s["turned"], HSEQ * h + j + 1)
                q = HSEQ * h + j
                nc.scalar.copy(xnT[:, q * SEQ:(q + 1) * SEQ], ps[:, j, :]).then_inc(s["xnT_ready"], 1)

            def lgT_out(h, j):
                act.wait_ge(s["routed"], HSEQ * h + j + 1)
                if HSEQ * h + j >= 2:
                    act.wait_ge(s["lg_turned"], HSEQ * h + j - 1)
                nc.scalar.copy(lgT[:, j % 2, :], ps[0:NR, 4 + j % 2, :]).then_inc(s["lgT_ready"], 1)

            for h in range(HALVES):
                xnT_out(h, 0)
                xnT_out(h, 1)
                lgT_out(h, 0)
                lgT_out(h, 1)
                xnT_out(h, 2)
                xnT_out(h, 3)
                lgT_out(h, 2)
                lgT_out(h, 3)
                act.wait_ge(s["lg_turned"], HSEQ * (h + 1))
                nc.scalar.activation(th_r[:, :, :], ps[:, 6, 0:HT * NR].rearrange("p (t r) -> p t r", r=NR),
                                     ACT.Tanh, scale=0.5).then_inc(s["scored"], 1)
                for j in range(HSEQ):
                    t = HT * h + TPS * j
                    nc.scalar.copy(rows[:, t:t + TPS, 0:P], xnb[:, TPS * j:TPS * (j + 1), :]).then_inc(s["rows_ready"], 1)

            act.wait_ge(s["bias0_ready"], 1)

            def rec_tanh(q, par):
                act.wait_ge(s["rec_mm"], q + 1)
                wait(act, "rec_scan", q - 1)
                nc.scalar.activation(tg[:, par, :], ps[:, 3 * par, :], ACT.Tanh, bias=a0bh[:, 0:1], scale=0.5)
                nc.scalar.activation(tv[:, par, :], ps[:, 3 * par + 1, :], ACT.Tanh, bias=a0b[:, 1:2])
                nc.scalar.activation(td[:, par, :], ps[:, 3 * par + 2, :], ACT.Tanh, bias=a0bh[:, 2:3],
                                     scale=0.5).then_inc(s["rec_act"], 1)

            def rec_out(q, par):
                act.wait_ge(s["rec_turned"], q + 1)
                nc.scalar.copy(seq_of(sT, q), ps[:, 6 + par, :].rearrange("p (t d) -> p t d", d=P)).then_inc(s["rec_out"], 1)

            def rec_pair(i):
                rec_tanh(2 * i, 0)
                if not (isinstance(i, int) and i == 0):
                    rec_out(2 * i - 1, 1)
                rec_tanh(2 * i + 1, 1)
                rec_out(2 * i, 0)

            rec_pair(0)
            with act.Fori(1, SEQS // 2) as i:
                rec_pair(i)
            rec_out(SEQS - 1, 1)

            def sxT_out(n, par):
                act.wait_ge(s["f_turned"], n + 1)
                nc.scalar.copy(sxT[:, par, :], ps[:, 7, 0:P]).then_inc(s["f_xT"], 1)

            def gate_tanh(n, par):
                act.wait_ge(s["f_gate"], n + 1)
                nc.scalar.activation(th0[:, par, :], ps[:, par, :], ACT.Tanh, scale=0.5).then_inc(s["f_th"], 1)

            def h0T_out(n, par):
                act.wait_ge(s["f_hT"], n + 1)
                nc.scalar.copy(h0T[:, par, :], ps[:, 4 + par, :]).then_inc(s["f_hTs"], 1)

            def experts0_slot(n, par, before=1, after=1):
                gate_tanh(n, par)
                if after:
                    sxT_out(n + 1, 1 - par)
                if before:
                    h0T_out(n - 1, 1 - par)

            sxT_out(0, 0)
            experts0_slot(0, 0, before=0)
            experts0_slot(1, 1)
            with act.Fori(1, SORTED // 2 - 1) as i:
                experts0_slot(2 * i, 0)
                experts0_slot(2 * i + 1, 1)
            experts0_slot(SORTED - 2, 0)
            experts0_slot(SORTED - 1, 1, after=0)
            h0T_out(SORTED - 1, 1)

            def front(k, u):
                if u == 0:
                    act.wait_ge(s["gathered"], 16 * TPS * (k + 1))
                    nc.scalar.activation(thy[:, :].rearrange("p (t d) -> p t d", d=P), seq_of(ya, k),
                                         ACT.Tanh, scale=0.5).then_inc(s["c_th"], 1)
                if u == 10:
                    act.wait_ge(s["c_turned"], k + 1)
                    wait(act, "c_copy", TPS * k)
                    nc.scalar.copy(xn1T[:, :], ps[:, 4, :]).then_inc(s["c_xT"], 1)
                for i, (at_u, name) in enumerate(((13, "c_q"), (14, "c_k"))):
                    if u == at_u:
                        act.wait_ge(s[name], k + 1)
                        nc.scalar.activation(expq[:, i, :], ps[:, 5 + i, :], ACT.Exp, bias=a1b[:, i:i + 1])
                        nc.scalar.activation(linq[:, i, :], ps[:, 5 + i, :], ACT.Identity,
                                             bias=a1b1[:, i:i + 1]).then_inc(s["c_lin"], 1)
                if u == 15:
                    act.wait_ge(s["c_lgm"], k + 1)
                    nc.scalar.activation(e1[:, :, :], lg[:, :, :], ACT.Exp).then_inc(s["c_exp"], 1)

            def unit_tanh(j, u):
                t, p = divmod(u, UNITS)
                n = USEQ * j + u
                if u == 0:
                    act.wait_ge(s["c_scores"], j + 1)
                act.wait_ge(s["m_gu"], n + 1)
                bank = ps[:, u % 2, :]
                if p < PAIRS:
                    for e in range(2):
                        last = nc.scalar.activation(th1[:, u % 2, e * P:(e + 1) * P], bank[:, e * P:(e + 1) * P],
                                                    ACT.Tanh, scale=half_s[:, t, 2 * p + e:2 * p + e + 1])
                else:
                    last = nc.scalar.activation(th1[:, u % 2, 0:P], bank[:, 0:P], ACT.Tanh, scale=0.5)
                last.then_inc(s["m_th"], 1)

            def unit_hT(j, u):
                n = USEQ * j + u
                w = 2 * P if u % UNITS < PAIRS else P
                act.wait_ge(s["m_hT"], n + 1)
                nc.scalar.copy(h1T[:, u % 2, 0:w], ps[:, 2, 0:w]).then_inc(s["m_hTs"], 1)

            def final_tanh(j, t):
                act.wait_ge(s["m_y"], USEQ * j + UNITS * (t + 1))
                nc.scalar.activation(thf[:, t % 2, :], ps[:, 3, 0:P], ACT.Tanh, scale=0.5).then_inc(s["m_thf"], 1)

            def step(k, fronts=True, tiles=True):
                for u in range(USEQ):
                    if tiles:
                        unit_tanh(k - 1, u)
                        if u >= 2:
                            unit_hT(k - 1, u - 2)
                        if u >= UNITS + 2 and (u - 2) % UNITS == 0:
                            final_tanh(k - 1, (u - 2) // UNITS - 1)
                    if fronts:
                        front(k, u)
                if tiles:
                    unit_hT(k - 1, USEQ - 2)
                    unit_hT(k - 1, USEQ - 1)
                    final_tanh(k - 1, TPS - 1)

            act.wait_ge(s["bias1_ready"], 1)
            step(0, tiles=False)
            with act.Fori(1, SEQS) as k:
                step(k)
            step(SEQS, fronts=False)

        @block.tensor
        def _(pe):
            pe.wait_ge(s["consts_in"], 32)

            def turn_xn(h, j):
                pe.wait_ge(s["normed"], HSEQ * h + j + 1)
                for t in range(TPS):
                    last = pe.transpose(ps[:, j, t * P:(t + 1) * P], xnb[:, TPS * j + t, :], ident)
                last.then_inc(s["turned"], 1)

            def route(h, j):
                q = HSEQ * h + j
                pe.wait_ge(s["xnT_ready"], q + 1)
                if q >= 2:
                    pe.wait_ge(s["lgT_ready"], q - 1)
                pe.matmul(ps[0:NR, 4 + j % 2, :], r0[:, :], xnT[:, q * SEQ:(q + 1) * SEQ],
                          start=True, stop=True).then_inc(s["routed"], 1)

            def turn_logits(h, j):
                pe.wait_ge(s["lgT_ready"], HSEQ * h + j + 1)
                if h > 0 and j == 0:
                    pe.wait_ge(s["scored"], h)
                for t in range(TPS):
                    c = (TPS * j + t) * NR
                    last = pe.transpose(ps[:, 6, c:c + NR], lgT[:, j % 2, t * P:(t + 1) * P], ident[0:NR, 0:NR])
                last.then_inc(s["lg_turned"], 1)

            for h in range(HALVES):
                turn_xn(h, 0)
                turn_xn(h, 1)
                route(h, 0)
                route(h, 1)
                turn_xn(h, 2)
                turn_xn(h, 3)
                turn_logits(h, 0)
                turn_logits(h, 1)
                route(h, 2)
                route(h, 3)
                turn_logits(h, 2)
                turn_logits(h, 3)
                pe.wait_ge(s["counted"], h + 1)
                pe.matmul(ps[:, 7, 0:GROUPS], lower, cum[:, :, HT - 1], start=True, stop=True)
                pe.matmul(ps[:, 7, GROUPS:2 * GROUPS], ones, cum[:, :, HT - 1], start=True, stop=True).then_inc(s["placed"], 1)

            pe.wait_ge(s["attn0_in"], 32)

            def rec_project(q, par):
                wait(pe, "rec_act", q - 1)
                for i in range(3):
                    last = pe.matmul(ps[:, 3 * par + i, :], a0w[:, i * P:(i + 1) * P],
                                     xnT[:, bass.ds(q * SEQ, SEQ)], start=True, stop=True)
                last.then_inc(s["rec_mm"], 1)

            def rec_turn(q, par):
                pe.wait_ge(s["rec_scan"], q + 1)
                for t in range(TPS):
                    last = pe.transpose(ps[:, 6 + par, t * P:(t + 1) * P], scan[:, par, t * P:(t + 1) * P], ident)
                last.then_inc(s["rec_turned"], 1)

            def rec_pair(i):
                rec_project(2 * i, 0)
                if not (isinstance(i, int) and i == 0):
                    rec_turn(2 * i - 1, 1)
                rec_project(2 * i + 1, 1)
                rec_turn(2 * i, 0)

            rec_pair(0)
            with pe.Fori(1, SEQS // 2) as i:
                rec_pair(i)
            rec_turn(SEQS - 1, 1)

            pe.wait_ge(s["rec_out"], SEQS)
            pe.wait_ge(s["attn1_in"], 16 * 4)
            pe.wait_ge(s["bias1_ready"], 1)
            pe.matmul(ps[:, 6, 0:P], a1w[:, 2 * P:3 * P], wo[:, :], start=True, stop=True)
            pe.matmul(ps[:, 6, P:2 * P], bv_cols[:, :], wo[:, :], start=True, stop=True).then_inc(s["fused"], 1)

            pe.wait_ge(s["experts0_in"], 16)
            pe.wait_ge(s["group_ready"], HALVES)
            at_hand = [pe.alloc_register(f"at_hand{par}") for par in range(2)]
            behind = [pe.alloc_register(f"behind{par}") for par in range(2)]

            def group_of(reg):
                return pe.snap(reg, min_val=0, max_val=(GROUPS - 1) * W0)

            def turn_rows(n, par):
                pe.wait_ge(s["f_row"], n + 1)
                pe.transpose(ps[:, 7, 0:P], srow[:, par, 0:P], ident).then_inc(s["f_turned"], 1)

            def gate(n, par):
                g = group_of(at_hand[par])
                pe.wait_ge(s["f_xT"], n + 1)
                pe.matmul(ps[:, par, :], sxT[:, par, :], w0s[:, bass.ds(g, GU0)],
                          start=True, stop=True).then_inc(s["f_gate"], 1)

            def up(n, par):
                g = group_of(at_hand[par])
                pe.matmul(ps[:, 2 + par, :], sxT[:, par, :], w0s[:, bass.ds(g + GU0, GU0)],
                          start=True, stop=True).then_inc(s["f_up"], 1)

            def turn_h0(n, par):
                pe.wait_ge(s["f_h"], n + 1)
                for c in range(HC):
                    last = pe.transpose(ps[:, 4 + par, c * P:(c + 1) * P], h0[:, par, c * P:(c + 1) * P], ident)
                last.then_inc(s["f_hT"], 1)

            def down(n, par):
                g = group_of(behind[par])
                pe.wait_ge(s["f_hTs"], n + 1)
                wait(pe, "f_y", n)
                for c in range(HC):
                    last = pe.matmul(ps[:, 6, 0:P], h0T[:, par, c * P:(c + 1) * P],
                                     w0s[:, bass.ds(g + 2 * GU0 + c * P, P)], start=(c == 0), stop=(c == HC - 1))
                last.then_inc(s["f_down"], 1)

            def experts0_slot(n, par, before=2, after=1):
                gate(n, par)
                if before > 1:
                    down(n - 2, par)
                pe.reg_mov(behind[par], at_hand[par])
                if after:
                    turn_rows(n + 1, 1 - par)
                up(n, par)
                if after:
                    pe.reg_load(at_hand[1 - par], group[0:1, bass.ds(n + 1, 1)])
                if before > 0:
                    turn_h0(n - 1, 1 - par)

            pe.reg_load(at_hand[0], group[0:1, 0:1])
            turn_rows(0, 0)
            pe.wait_ge(s["fused_out"], 1)
            experts0_slot(0, 0, before=0)
            experts0_slot(1, 1, before=1)
            with pe.Fori(1, SORTED // 2 - 1) as i:
                experts0_slot(2 * i, 0)
                experts0_slot(2 * i + 1, 1)
            experts0_slot(SORTED - 2, 0)
            experts0_slot(SORTED - 1, 1, after=0)
            down(SORTED - 2, 0)
            turn_h0(SORTED - 1, 1)
            down(SORTED - 1, 1)

            pe.wait_ge(s["experts1_in"], 16 * 3)
            pe.wait_ge(s["f_y"], SORTED)

            def front(k, u):
                if u == 9:
                    pe.wait_ge(s["c_xn"], k + 1)
                    for t in range(TPS):
                        last = pe.transpose(ps[:, 4, t * P:(t + 1) * P], xn1[:, t, :], ident)
                    last.then_inc(s["c_turned"], 1)
                if u == 11:
                    pe.wait_ge(s["c_xT"], k + 1)
                    wait(pe, "c_s1", k)
                    pe.matmul(ps[:, 5, :], a1w[:, 0:P], xn1T[:, :], start=True, stop=True).then_inc(s["c_q"], 1)
                if u == 12:
                    pe.matmul(ps[:, 6, :], a1w[:, P:2 * P], xn1T[:, :], start=True, stop=True).then_inc(s["c_k"], 1)
                    for t in range(TPS):
                        o = (t % 2) * (P + E1)
                        last = pe.matmul(ps[:, 7 if t < 2 else 4, o:o + P + E1], xn1T[:, t * P:(t + 1) * P], vg_w[:, :],
                                         start=True, stop=True)
                    last.then_inc(s["c_v"], 1)

            def scores(k, sr):
                bank = (5, 6, 7, 4)[sr]
                if sr == 0:
                    pe.wait_ge(s["c_qkT"], 2 * (k + 1))
                    pe.wait_ge(s["c_lg"], k + 1)
                pe.matmul(ps[:, bank, 0:SEQ - sr * P], kT[:, sr * P:(sr + 1) * P], qT[:, sr * P:SEQ],
                          start=True, stop=True).then_inc(s["c_a"], 1)

            def attend(j):
                pe.wait_ge(s["c_at"], TPS * (j + 1))
                for c in range(TPS):
                    o = (c % 2) * (P + 1)
                    for sr in range(c + 1):
                        last = pe.matmul(ps[:, 5 + c // 2, o:o + P + 1], at[:, sr, c * P:(c + 1) * P], vo[:, sr, :],
                                         start=(sr == 0), stop=(sr == c))
                last.then_inc(s["c_num"], 1)

            def unit_gu(j, u):
                t, p = divmod(u, UNITS)
                w = 4 * P if p < PAIRS else 2 * P
                if p == 0:
                    pe.wait_ge(s["c_copy"], TPS * j + t + 1)
                if u >= 2:
                    pe.wait_ge(s["m_h"], USEQ * j + u - 1)
                pe.matmul(ps[:, u % 2, 0:w], xc[:, t, :], w13s[:, 4 * P * p:4 * P * p + w],
                          start=True, stop=True).then_inc(s["m_gu"], 1)

            def unit_turn(j, u):
                n = USEQ * j + u
                pe.wait_ge(s["m_h"], n + 1)
                if u > 0:
                    pe.wait_ge(s["m_hTs"], n)
                for e in range(2 if u % UNITS < PAIRS else 1):
                    last = pe.transpose(ps[:, 2, e * P:(e + 1) * P], h1[:, u % 2, e * P:(e + 1) * P], ident)
                last.then_inc(s["m_hT"], 1)

            def unit_down(j, u):
                t, p = divmod(u, UNITS)
                n = USEQ * j + u
                pe.wait_ge(s["m_hTs"], n + 1)
                if p == 0:
                    pe.wait_ge(s["m_gf"], 1 + TPS * j + t)
                for e in range(2 if p < PAIRS else 1):
                    last = pe.matmul(ps[:, 3, 0:P], h1T[:, u % 2, e * P:(e + 1) * P],
                                     w2s[:, (2 * p + e) * P:(2 * p + e + 1) * P],
                                     start=(p == 0 and e == 0), stop=(p == PAIRS))
                last.then_inc(s["m_y"], 1)

            def step(k, fronts=True, tiles=True):
                for u in range(USEQ):
                    if tiles:
                        unit_gu(k - 1, u)
                        if u == 1:
                            attend(k - 1)
                        if u >= 2:
                            unit_turn(k - 1, u - 2)
                        if u >= 3:
                            unit_down(k - 1, u - 3)
                    if fronts:
                        front(k, u)
                if fronts:
                    scores(k, 0)
                    scores(k, 1)
                if tiles:
                    unit_turn(k - 1, USEQ - 2)
                    unit_down(k - 1, USEQ - 3)
                if fronts:
                    scores(k, 2)
                    scores(k, 3)
                if tiles:
                    unit_turn(k - 1, USEQ - 1)
                    unit_down(k - 1, USEQ - 2)
                    unit_down(k - 1, USEQ - 1)

            step(0, tiles=False)
            with pe.Fori(1, SEQS) as k:
                step(k)
            step(SEQS, fronts=False)

        @block.vector
        def _(dve):
            chain = [0]

            def link(ins):
                chain[0] += 1
                ins.then_inc(s["chain"], 1)
                dve.wait_ge(s["chain"], chain[0])

            nc.vector.memset(dummy[:, :], 0.0).then_inc(s["dummy_set"], 1)
            dve.sem_inc(s["m_gf"], 1)
            for par in range(2):
                dve.sem_inc(o_stored[par], FREE)

            def stats(h):
                dve.wait_ge(s["x_in"], 16 * HSEQ * (h + 1))
                for i in range(2):
                    r = range(2 * TPS * i, 2 * TPS * (i + 1))
                    for t in r:
                        last = nc.vector.bn_stats(st[:, t, :], xa[:, HT * h + t, :])
                    link(last)
                    for t in r:
                        last = nc.vector.bn_aggr(mv[:, t, :], st[:, t, :])
                    link(last)
                    nc.vector.tensor_scalar(var[:, r.start:r.stop], mv[:, r.start:r.stop, 1], LN_EPS, None,
                                            ALU.add).then_inc(s["vars"], 1)

            def normalise(h):
                if h > 0:
                    dve.wait_ge(s["turned"], HSEQ * h)
                    dve.wait_ge(s["rows_ready"], HSEQ * h)
                for j in range(HSEQ):
                    if j % 2 == 0:
                        dve.wait_ge(s["rstds"], 2 * h + j // 2 + 1)
                    for t in range(TPS * j, TPS * (j + 1)):
                        last = nc.vector.tensor_scalar(xnb[:, t, :], xa[:, HT * h + t, :], mv[:, t, 0:1], rstd[:, t:t + 1],
                                                       ALU.subtract, ALU.mult)
                    last.then_inc(s["normed"], 1)

            def slots(h):
                dve.wait_ge(s["scored"], h + 1)
                link(nc.vector.tensor_scalar(sc_r[:, :, :], th_r[:, :, :], 0.5, 0.5, ALU.mult, ALU.add))
                macro = sc_r[:, :, 0:GROUPS]
                micro = sc_r[:, :, GROUPS:NR].rearrange("p t (g e) -> p t g e", e=EPG)
                to_groups = [P, HT, GROUPS]
                link(nc.vector.tensor_reduce(best[:, :], macro, AX_X, ALU.max))
                link(nc.vector.tensor_tensor(ohg[:, :, :], macro, best[:, :].unsqueeze(2).broadcast_to(to_groups), ALU.is_ge))
                link(nc.vector.tensor_tensor(ohg[:, :, :], ohg[:, :, :],
                                             fall[:, E1 - GROUPS:E1].unsqueeze(1).broadcast_to(to_groups), ALU.mult))
                link(nc.vector.tensor_reduce(best_e[:, :], ohg[:, :, :], AX_X, ALU.max))
                link(nc.vector.tensor_tensor(ohg[:, :, :], ohg[:, :, :],
                                             best_e[:, :].unsqueeze(2).broadcast_to(to_groups), ALU.is_equal))
                if h > 0:
                    dve.wait_ge(s["placed"], h)
                for g in range(GROUPS):
                    last = nc.vector.tensor_tensor_scan(cum[:, g, :], ones[:, 0:HT], ohg[:, :, g], 0.0, ALU.mult, ALU.add)
                last.then_inc(s["counted"], 1)
                link(nc.vector.tensor_tensor(usum[:, :, :], micro[:, :, :, 0], micro[:, :, :, 1], ALU.add))
                link(nc.vector.tensor_scalar(usum[:, :, :], usum[:, :, :], TOPK_EPS, None, ALU.add))
                link(nc.vector.reciprocal(usum[:, :, :], usum[:, :, :]))
                link(nc.vector.tensor_scalar(mfac[:, :], best[:, :], TOPK_EPS, None, ALU.add))
                link(nc.vector.reciprocal(mfac[:, :], mfac[:, :]))
                link(nc.vector.tensor_tensor(mfac[:, :], mfac[:, :], best[:, :], ALU.mult))
                link(nc.vector.tensor_tensor(usum[:, :, :], usum[:, :, :],
                                             mfac[:, :].unsqueeze(2).broadcast_to(to_groups), ALU.mult))
                link(nc.vector.tensor_tensor(usum[:, :, :], usum[:, :, :], ohg[:, :, :], ALU.mult))
                link(nc.vector.tensor_tensor(uw[:, :, :, :], micro,
                                             usum[:, :, :].unsqueeze(3).broadcast_to([P, HT, GROUPS, EPG]), ALU.mult))
                nc.vector.tensor_reduce(rows[:, HT * h:HT * (h + 1), P:ROW], uw[:, :, :, :].rearrange("p t g e -> p t e g"),
                                        AX_X, ALU.add)
                dve.wait_ge(s["placed"], h + 1)
                link(nc.vector.tensor_copy(tot[:, :], ps[:, 7, 0:2 * GROUPS]))
                link(nc.vector.tensor_scalar(ntile[:, :], tot[:, GROUPS:2 * GROUPS], 1.0 / P, (P / 2 - 0.5) / P,
                                             ALU.mult, ALU.add))
                link(nc.vector.tensor_scalar(ntile[:, :], ntile[:, :], MAGIC, MAGIC, ALU.add, ALU.subtract))
                link(nc.vector.tensor_tensor_scan(ends[:, :], ones[:, 0:GROUPS], ntile[:, :], 0.0, ALU.mult, ALU.add))
                link(nc.vector.tensor_tensor(base[:, :], ends[:, :], ntile[:, :], ALU.subtract))
                link(nc.vector.scalar_tensor_tensor(base[:, :], base[:, :], float(P), tot[:, 0:GROUPS], ALU.mult, ALU.add))
                link(nc.vector.tensor_scalar(base[:, :], base[:, :], float(h * FT * P - 1), None, ALU.add))
                link(nc.vector.tensor_tensor(where[:, :, :], cum[:, :, :],
                                             base[:, :].unsqueeze(2).broadcast_to([P, GROUPS, HT]), ALU.add))
                link(nc.vector.tensor_tensor(where[:, :, :], where[:, :, :], ohg[:, :, :].rearrange("p t g -> p g t"), ALU.mult))
                link(nc.vector.tensor_reduce(slot_f[:, :], where[:, :, :].rearrange("p g t -> p t g"), AX_X, ALU.add))
                nc.vector.tensor_copy(slot[:, HT * h:HT * (h + 1)], slot_f[:, :]).then_inc(s["slots_ready"], 1)
                link(nc.vector.tensor_tensor(past[0:1, :, :],
                                             cst[0:1, C_TILE:C_TILE + FT].unsqueeze(2).broadcast_to([1, FT, GROUPS - 1]),
                                             ends[0:1, 0:GROUPS - 1].unsqueeze(1).broadcast_to([1, FT, GROUPS - 1]), ALU.is_ge))
                link(nc.vector.tensor_reduce(group_f[:, :], past[0:1, :, :], AX_X, ALU.add))
                link(nc.vector.tensor_scalar(group_f[:, :], group_f[:, :], float(W0), None, ALU.mult))
                nc.vector.tensor_copy(group[:, FT * h:FT * (h + 1)], group_f[:, :]).then_inc(s["group_ready"], 1)

            stats(0)
            normalise(0)
            stats(1)
            dve.wait_ge(s["consts_in"], 32)
            slots(0)
            normalise(1)
            dve.wait_ge(s["attn0_in"], 32)
            nc.vector.tensor_scalar(a0bh[:, :], a0b[:, :], 0.5, None, ALU.mult).then_inc(s["bias0_ready"], 1)
            dve.wait_ge(s["attn1_in"], 16 * 4)
            nc.vector.tensor_scalar(a1b1[:, :], a1b[:, 0:2], 1.0, None, ALU.add)
            nc.vector.tensor_scalar(bv_cols[:, :], ones, a1b[:, 2:3], None, ALU.mult).then_inc(s["bias1_ready"], 1)
            slots(1)

            def rec_scan(q, par):
                dve.wait_ge(s["rec_act"], q + 1)
                nc.vector.tensor_scalar(td[:, par, :], td[:, par, :], 0.499, 0.5, ALU.mult, ALU.add).then_inc(s["rec_x"], 1)
                nc.vector.scalar_tensor_tensor(tg[:, par, :], tg[:, par, :], 1.0, tv[:, par, :],
                                               ALU.add, ALU.mult).then_inc(s["rec_x"], 1)
                dve.wait_ge(s["rec_x"], 2 * q + 2)
                wait(dve, "rec_turned", q - 1)
                nc.vector.tensor_tensor_scan(scan[:, par, :], td[:, par, :], tg[:, par, :], 0.0,
                                             ALU.mult, ALU.add).then_inc(s["rec_scan"], 1)

            def rec_pair(i):
                rec_scan(2 * i, 0)
                rec_scan(2 * i + 1, 1)

            rec_pair(0)
            with dve.Fori(1, SEQS // 2) as i:
                rec_pair(i)

            dve.wait_ge(s["fused"], 1)
            nc.vector.tensor_copy(vg_w[:, 0:P], ps[:, 6, 0:P])
            nc.vector.tensor_copy(bv_wo[:, :], ps[:, 6, P:2 * P]).then_inc(s["fused_out"], 1)

            def weights(n, par):
                dve.wait_ge(s["f_row"], n + 1)
                wait(dve, "f_h", n - 1)
                nc.vector.tensor_scalar(sw[:, par, :], srow[:, par, P:ROW], 0.5, None,
                                        ALU.mult).then_inc(s["f_w"], 1)

            def hidden(n, par):
                dve.wait_ge(s["f_th"], n + 1)
                wait(dve, "f_hT", n - 1)
                nc.vector.scalar_tensor_tensor(h0[:, par, :], th0[:, par, :], 1.0, ps[:, par, :],
                                               ALU.add, ALU.mult).then_inc(s["f_a"], 1)
                dve.wait_ge(s["f_a"], n + 1)
                dve.wait_ge(s["f_w"], n + 1)
                dve.wait_ge(s["f_up"], n + 1)
                for e in range(EPG):
                    c = slice(e * F0, (e + 1) * F0)
                    last = nc.vector.scalar_tensor_tensor(h0[:, par, c], h0[:, par, c], sw[:, par, e:e + 1],
                                                          ps[:, 2 + par, c], ALU.mult, ALU.mult)
                last.then_inc(s["f_h"], 1)

            def result(n):
                dve.wait_ge(s["f_down"], n + 1)
                nc.vector.tensor_copy(tile_at(sorted_sb, n)[:, 0:P], ps[:, 6, 0:P]).then_inc(s["f_y"], 1)

            def experts0_slot(n, par, before=2, after=1):
                if after:
                    weights(n + 1, 1 - par)
                if before > 1:
                    result(n - 2)
                hidden(n, par)

            weights(0, 0)
            experts0_slot(0, 0, before=0)
            experts0_slot(1, 1, before=1)
            with dve.Fori(1, SORTED // 2 - 1) as i:
                experts0_slot(2 * i, 0)
                experts0_slot(2 * i + 1, 1)
            experts0_slot(SORTED - 2, 0)
            experts0_slot(SORTED - 1, 1, after=0)
            result(SORTED - 2)
            result(SORTED - 1)

            R_AT = (1, 1, 1, 0, 1, 1, 0, 0, 0, 0, 0, 0, 0, 1, 0, 0, 3, 5, 6, 2)
            R_STEPS = sum(R_AT)

            def front(k, u):
                n = [R_STEPS * k + sum(R_AT[:u])]

                def then(ins):
                    n[0] = n[0] + 1
                    ins.then_inc(s["c_chain"], 1)
                    dve.wait_ge(s["c_chain"], n[0])

                by_expert = [P, TPS, E1]
                g3 = gy[:, :].rearrange("p (t d) -> p t d", d=P)
                if u == 0:
                    dve.wait_ge(s["c_th"], k + 1)
                    then(nc.vector.scalar_tensor_tensor(g3, thy[:, :].rearrange("p (t d) -> p t d", d=P), 1.0,
                                                        seq_of(ya, k), ALU.add, ALU.mult))
                if u == 1:
                    then(nc.vector.tensor_tensor(g3, g3, seq_of(sT, k), ALU.mult))
                if u == 2:
                    then(nc.vector.scalar_tensor_tensor(seq_of(xa, k), g3, 0.25, seq_of(xa, k), ALU.mult, ALU.add))
                if u == 4:
                    for t in range(TPS):
                        last = nc.vector.bn_stats(st1[:, t, :], xa[:, bass.ds(k * TPS + t, 1), :].rearrange("p o d -> p (o d)"))
                    then(last)
                if u == 5:
                    for t in range(TPS):
                        last = nc.vector.bn_aggr(mv1[:, t, :], st1[:, t, :])
                    then(last)
                    nc.vector.tensor_scalar(var1[:, :], mv1[:, :, 1], LN_EPS, None, ALU.add).then_inc(s["c_var"], 1)
                if u == 8:
                    dve.wait_ge(s["c_rstd"], k + 1)
                    for t in range(TPS):
                        last = nc.vector.tensor_scalar(xn1[:, t, :], xa[:, bass.ds(k * TPS + t, 1), :].rearrange("p o d -> p (o d)"),
                                                       mv1[:, t, 0:1], rstd1[:, t:t + 1], ALU.subtract, ALU.mult)
                    last.then_inc(s["c_xn"], 1)
                if u == 13:
                    dve.wait_ge(s["c_v"], k + 1)
                    for i, bank in enumerate((7, 4)):
                        two = ps[:, bank, 0:2 * (P + E1)].rearrange("p (t c) -> p t c", c=P + E1)
                        nc.vector.tensor_tensor(vo[:, 2 * i:2 * i + 2, 0:P], two[:, :, 0:P],
                                                bv_wo[:, :].unsqueeze(1).broadcast_to([P, 2, P]), ALU.add)
                        last = nc.vector.tensor_copy(lg[:, 2 * i:2 * i + 2, :], two[:, :, P:P + E1])
                    last.then_inc(s["c_lg"], 1)
                    dve.wait_ge(s["c_lg"], k + 1)
                    then(nc.vector.tensor_reduce(rm[:, :], lg[:, :, :], AX_X, ALU.max))
                    nc.vector.tensor_tensor(lg[:, :, :], lg[:, :, :], rm[:, :].unsqueeze(2).broadcast_to(by_expert),
                                            ALU.subtract).then_inc(s["c_lgm"], 1)
                for i, at_u in enumerate((14, 15)):
                    if u == at_u:
                        dve.wait_ge(s["c_lin"], 2 * k + i + 1)
                        nc.vector.scalar_tensor_tensor((qT, kT)[i][:, :], expq[:, i, :], 1.0, linq[:, i, :],
                                                       ALU.min, ALU.max).then_inc(s["c_qkT"], 1)
                if u == 16:
                    dve.wait_ge(s["c_exp"], k + 1)
                    then(nc.vector.tensor_reduce(rs[:, :], e1[:, :, :], AX_X, ALU.add))
                    then(nc.vector.reciprocal(rs[:, :], rs[:, :]))
                    then(nc.vector.tensor_tensor(pr[:, :, :], e1[:, :, :], rs[:, :].unsqueeze(2).broadcast_to(by_expert), ALU.mult))
                for at_u, src, oh in ((17, pr, oh1), (18, rq, oh2)):
                    if u == at_u:
                        if oh is oh2:
                            then(nc.vector.scalar_tensor_tensor(rq[:, :, :], oh1[:, :, :], -2.0, pr[:, :, :], ALU.mult, ALU.add))
                        then(nc.vector.tensor_reduce(rm[:, :], src[:, :, :], AX_X, ALU.max))
                        then(nc.vector.tensor_tensor(oh[:, :, :], src[:, :, :], rm[:, :].unsqueeze(2).broadcast_to(by_expert), ALU.is_ge))
                        then(nc.vector.tensor_tensor(oh[:, :, :], oh[:, :, :], fall.unsqueeze(1).broadcast_to(by_expert), ALU.mult))
                        then(nc.vector.tensor_reduce(rs[:, :], oh[:, :, :], AX_X, ALU.max))
                        then(nc.vector.tensor_tensor(oh[:, :, :], oh[:, :, :], rs[:, :].unsqueeze(2).broadcast_to(by_expert), ALU.is_equal))
                if u == 19:
                    then(nc.vector.tensor_tensor(oh1[:, :, :], oh1[:, :, :], oh2[:, :, :], ALU.add))
                    then(nc.vector.tensor_tensor(pr[:, :, :], pr[:, :, :], oh1[:, :, :], ALU.mult))
                assert not isinstance(k, int) or n[0] == R_STEPS * k + sum(R_AT[:u + 1]), (u, n)

            def scaled_scores(k):
                nc.vector.tensor_scalar(half_s[:, :, :], pr[:, :, :], 0.5, None, ALU.mult)
                nc.vector.scalar_tensor_tensor(half_s2[:, :, :], pr[:, :, :], 0.5, pr[:, :, :],
                                               ALU.mult, ALU.mult).then_inc(s["c_scores"], 1)

            def masked(k, sr):
                dve.wait_ge(s["c_a"], TPS * k + sr + 1)
                w = SEQ - sr * P
                nc.vector.tensor_tensor(at[:, sr, sr * P:SEQ], ps[:, (5, 6, 7, 4)[sr], 0:w], cst[:, C_CAUSAL:C_CAUSAL + w],
                                        ALU.mult).then_inc(s["c_at"], 1)

            def attention(j):
                dve.wait_ge(s["c_num"], j + 1)
                for i in range(2):
                    nc.vector.tensor_scalar(den[:, 2 * i:2 * i + 2],
                                            ps[:, 5 + i, 0:2 * (P + 1)].rearrange("p (t c) -> p t c", c=P + 1)[:, :, P],
                                            ATT_EPS, None, ALU.add).then_inc(s["c_den"], 1)
                dve.wait_ge(s["c_den"], 3 * j + 2)
                nc.vector.reciprocal(den[:, :], den[:, :]).then_inc(s["c_den"], 1)
                dve.wait_ge(s["c_den"], 3 * j + 3)
                for c in range(TPS):
                    o = (c % 2) * (P + 1)
                    last = nc.vector.scalar_tensor_tensor(s1[:, c, :], ps[:, 5 + c // 2, o:o + P], den[:, c:c + 1], bo[:, :],
                                                          ALU.mult, ALU.add)
                last.then_inc(s["c_s1"], 1)

            def unit(j, u):
                t, p = divmod(u, UNITS)
                n = USEQ * j + u
                w = 2 * P if p < PAIRS else P
                bank = ps[:, u % 2, :]
                dve.wait_ge(s["m_th"], n + 1)
                nc.vector.scalar_tensor_tensor(a1[:, u % 2, 0:w], th1[:, u % 2, 0:w], 1.0, bank[:, 0:w],
                                               ALU.add, ALU.mult).then_inc(s["m_a"], 1)
                dve.wait_ge(s["m_a"], n + 1)
                if u >= 2:
                    dve.wait_ge(s["m_hT"], n - 1)
                for e in range(w // P):
                    c = slice(e * P, (e + 1) * P)
                    last = nc.vector.scalar_tensor_tensor(
                        h1[:, u % 2, c], a1[:, u % 2, c], half_s2[:, t, 2 * p + e:2 * p + e + 1] if p < PAIRS else 0.5,
                        bank[:, w + e * P:w + (e + 1) * P], ALU.mult, ALU.mult)
                last.then_inc(s["m_h"], 1)

            def final(j, t):
                par = t % 2
                m = TPS * j + t
                dve.wait_ge(s["m_thf"], m + 1)
                nc.vector.scalar_tensor_tensor(gf[:, par, :], thf[:, par, :], 1.0, ps[:, 3, 0:P],
                                               ALU.add, ALU.mult).then_inc(s["m_gf"], 1)
                dve.wait_ge(s["m_gf"], 1 + m + 1)
                nc.vector.tensor_tensor(of[:, par, :], gf[:, par, :], s1[:, t, :], ALU.mult).then_inc(s["m_of"], 1)
                dve.wait_ge(s["m_of"], m + 1)
                dve.wait_ge(o_stored[par], FREE + 16 * (2 * j + t // 2))
                nc.vector.scalar_tensor_tensor(xo[:, par, :], of[:, par, :], 0.5,
                                               xa[:, bass.ds(m, 1), :].rearrange("p o d -> p (o d)"),
                                               ALU.mult, ALU.add).then_inc(s["m_xo"], 1)

            def step(k, fronts=True, tiles=True):
                for u in range(USEQ):
                    if tiles:
                        unit(k - 1, u)
                        if u == 3:
                            attention(k - 1)
                        if u >= UNITS + 2 and (u - 2) % UNITS == 0:
                            final(k - 1, (u - 2) // UNITS - 1)
                    if fronts:
                        front(k, u)
                if fronts:
                    scaled_scores(k)
                    for sr in range(TPS):
                        masked(k, sr)
                if tiles:
                    final(k - 1, TPS - 1)

            step(0, tiles=False)
            with dve.Fori(1, SEQS) as k:
                step(k)
            step(SEQS, fronts=False)


def kernel(**inputs):
    import numpy as np
    import concourse.bacc as bacc
    from concourse import mybir as mb
    from concourse.bass_utils import run_bass_kernel_spmd

    f = {k: np.asarray(v) for k, v in inputs.items()}
    cat = np.concatenate

    consts = np.zeros((P, CONSTS), np.float32)
    consts[:, C_ID:C_ID + P] = np.eye(P)
    consts[:, C_LOWER:C_LOWER + P] = np.triu(np.ones((P, P)), 1)
    consts[:, C_CAUSAL:C_CAUSAL + P] = np.triu(np.ones((P, P)))
    consts[:, C_ONES:C_FALL] = 1.0
    consts[:, C_FALL:C_FALL + E1] = np.arange(E1, 0, -1)
    consts[:, C_TILE:C_TILE + FT] = np.arange(FT)

    def columns(*names):
        return np.stack([f[n] for n in names], axis=1)

    ge = lambda w: w.reshape(GROUPS, EPG, P, F0).transpose(2, 0, 1, 3).reshape(P, GROUPS, EPG * F0)
    down = f["L0_ffn_down_w"].reshape(GROUPS, HC, P, P).transpose(2, 0, 1, 3).reshape(P, GROUPS, -1)
    experts0 = cat([ge(f["L0_ffn_gate_w"]), ge(f["L0_ffn_up_w"]), down], axis=2).reshape(P, -1)
    micro = f["L0_ffn_micro_w"].transpose(1, 0, 2).reshape(P, -1)
    pairs = lambda w: w.reshape(PAIRS, 2, P, P).transpose(2, 0, 1, 3).reshape(P, PAIRS, 2 * P)
    w13 = cat([cat([pairs(f["L1_ffn_w1"]), pairs(f["L1_ffn_w3"])], axis=2).reshape(P, -1),
               f["L1_ffn_w1s"][0], f["L1_ffn_w3s"][0], f["L1_ffn_gate_w"].T], axis=1)
    w2 = cat([f["L1_ffn_w2"].transpose(1, 0, 2).reshape(P, -1), f["L1_ffn_w2s"][0]], axis=1)
    arrays = {
        "x": f["L0_attn_x"],
        "consts": consts,
        "router0": cat([f["L0_ffn_macro_w"], micro], axis=1),
        "attn0_w": cat([f["L0_attn_Wg"].T, f["L0_attn_Wv"].T, f["L0_attn_Wd"].T], axis=1),
        "attn0_b": columns("L0_attn_bg", "L0_attn_bv", "L0_attn_bd"),
        "experts0": experts0,
        "attn1_w": cat([f["L1_attn_Wq"].T, f["L1_attn_Wk"].T, f["L1_attn_Wv"]], axis=1),
        "attn1_b": columns("L1_attn_bq", "L1_attn_bk", "L1_attn_bv"),
        "wo1": f["L1_attn_Wo"].T,
        "bo1": np.tile(f["L1_attn_bo"], (P, 1)),
        "w13": w13,
        "w2": w2,
    }
    nc = bacc.Bacc("TRN2", target_bir_lowering=False, num_devices=1)
    named, args = {}, []
    for name, a in arrays.items():
        a = np.ascontiguousarray(a)
        named[f"in_{name}"] = a
        args.append(nc.dram_tensor(f"in_{name}", a.shape, mb.dt.from_np(a.dtype), kind="ExternalInput").ap())
    args.append(nc.dram_tensor("out_x", arrays["x"].shape, mb.dt.from_np(arrays["x"].dtype), kind="ExternalOutput").ap())
    gated_recurrent_moe_two_layers(nc, *args)
    r = run_bass_kernel_spmd(nc, [named], core_ids=[0])
    return r.results[0]["out_x"]
```

```python
from contextlib import ExitStack

import concourse.bass as bass
from concourse import mybir

ALU = mybir.AluOpType
ACT = mybir.ActivationFunctionType
AX_X = mybir.AxisListType.X
F32 = mybir.dt.float32
I32 = mybir.dt.int32
U32 = mybir.dt.uint32
F32R = mybir.dt.float32r

P = 128
SEQS = 8
TPS = 4
SEQ = TPS * P
TILES = SEQS * TPS
HALVES = 2
HT = TILES // HALVES
HSEQ = SEQS // HALVES
GROUPS = 4
EPG = 2
F0 = 256
FT = HT + GROUPS - 1
SORTED = HALVES * FT
ROW = P + EPG
HC = EPG * F0 // P
E1 = 8
TOPK1 = 2
PAIRS = E1 // 2
W13 = 2 * E1 * P
UNITS = PAIRS + 1
USEQ = UNITS * TPS
GU0 = EPG * F0
D0 = HC * P
NR = GROUPS + GROUPS * EPG
RING = 3
BANKS = (0, 1, 7)
SCORE_BANKS = (6, 4, 5, 6)
EXP_AT = 13
DVE_TURNS = (12, 13)
LN_EPS = 1e-5
TOPK_EPS = 1e-9
ATT_EPS = 1e-6
MAGIC = float(1 << 23)

C_ID, C_LOWER, C_CAUSAL, C_ONES = (i * P for i in range(4))
C_FALL = C_CAUSAL + SEQ
C_TILE = C_FALL + E1
C_BEFORE = C_TILE + FT
CONSTS = C_BEFORE + E1 * E1


def gated_recurrent_moe_two_layers(
    nc, x, consts, router0, attn0_w, attn0_b, gate_up0, down0,
    attn1_w, attn1_b, wo1, bo1, w13, w2, out,
):
    ctx = ExitStack()
    with ctx:
        def sb(name, shape, dt=F32):
            return ctx.enter_context(nc.sbuf_tensor(name, shape, dt))

        def sem(name):
            return ctx.enter_context(nc.semaphore(name))

        sorted_rows = nc.dram_tensor("sorted_rows", [SORTED * P, ROW], F32, kind="Internal").ap()
        sorted_y = nc.dram_tensor("sorted_y", [SORTED * P, P], F32, kind="Internal").ap()
        x_t = x.rearrange("b (t p) d -> b p t d", p=P)
        out_t = out.rearrange("b (t p) d -> (b t) p d", p=P)
        rows_t = sorted_rows.rearrange("(n p) c -> p n c", p=P)
        y_t = sorted_y.rearrange("(n p) c -> p n c", p=P)

        ps = ctx.enter_context(nc.psum_tensor("ps", [P, 8, 512], F32))

        cst = sb("cst", [P, CONSTS])
        ident = cst[:, C_ID:C_ID + P]
        lower = cst[:, C_LOWER:C_LOWER + P]
        ones = cst[:, C_ONES:C_ONES + P]
        fall = cst[:, C_FALL:C_FALL + E1]
        r0 = sb("r0", [P, NR])
        a0w = sb("a0w", [P, 3 * P])
        a0b = sb("a0b", [P, 3])
        a0bh = sb("a0bh", [P, 3])
        w0d = sb("w0d", [P, GROUPS * D0])
        a1w = sb("a1w", [P, 3 * P])
        a1b = sb("a1b", [P, 3])
        a1bn = sb("a1bn", [P, 2])
        wo = sb("wo", [P, P])
        bo = sb("bo", [P, P])
        w13_shared = sb("w13_shared", [P, 2 * P])
        w2s = sb("w2s", [P, (E1 + 1) * P])
        vg_w = sb("vg_w", [P, P + E1])
        bv_wo = sb("bv_wo", [P, P])
        bv_cols = sb("bv_cols", [P, P])
        minus_half = sb("minus_half", [P, TPS])
        zero_rows = sb("zero_rows", [P, 2 * ROW])
        warm = sb("warm", [P, 1])

        xa = sb("xa", [P, TILES, P])
        xnT = sb("xnT", [P, SEQS * SEQ])
        sorted_sb = sb("sorted_sb", [P, FT + TILES, ROW])
        rows = sorted_sb[:, FT:FT + TILES, :]
        slot = sb("slot", [P, TILES], U32)
        group = sb("group", [1, SORTED], I32)
        sT = sb("sT", [P, TILES, P])
        ya = xnT[:, :].rearrange("p (t d) -> p t d", d=P)

        st = sb("st", [P, TILES, 6])
        mv = sb("mv", [P, TILES, 2])
        var = sb("var", [P, TILES])
        rstd = sb("rstd", [P, TILES])
        th_r = sb("th_r", [P, HT, NR])
        sc_r = sb("sc_r", [P, HT, NR])
        best = sb("best", [P, HT])
        best_e = sb("best_e", [P, HT])
        mfac = sb("mfac", [P, HT])
        ohg = sb("ohg", [P, HT, GROUPS])
        cum = sb("cum", [P, GROUPS, HT])
        cnt = sb("cnt", [P, GROUPS])
        tot = sb("tot", [P, 2 * GROUPS])
        ntile = sb("ntile", [P, GROUPS])
        ends = sb("ends", [P, GROUPS])
        base = sb("base", [P, GROUPS])
        where = sb("where", [P, GROUPS, HT])
        slot_f = sb("slot_f", [P, HT])
        group_f = sb("group_f", [1, FT])
        past = sb("past", [P, FT, GROUPS - 1])
        usum = sb("usum", [P, HT, GROUPS])
        uw = sb("uw", [P, HT, GROUPS, EPG])

        tg = sb("tg", [P, 2, SEQ])
        tv = sb("tv", [P, 2, SEQ])

        srow = sb("srow", [P, 2, ROW])
        sw = sb("sw", [P, 2, EPG])
        sx_round = sb("sx_round", [P, 2, P], F32R)
        sx_rest = sb("sx_rest", [P, 2, P], F32R)
        dummy = sb("first_act", [P, 2])
        h0 = sb("h0", [P, 2, 512])
        h0T = sb("h0T", [P, 2, 512])

        gy = sb("gy", [P, SEQ])
        st1 = sb("st1", [P, TPS, 6])
        mv1 = sb("mv1", [P, TPS, 2])
        var1 = sb("var1", [P, TPS])
        rstd1 = sb("rstd1", [P, TPS])
        xn1 = sb("xn1", [P, TPS, P])
        xn1T = sb("xn1T", [P, SEQ])
        xc = sb("xc", [P, TPS, P])
        exp_qk, relu_qk = tg, tv
        qT = sb("qT", [P, SEQ])
        kT = sb("kT", [P, SEQ])
        vo = sb("vo", [P, TPS, P + 1])
        lg = sb("lg", [P, TPS, E1])
        e1 = sb("e1", [P, TPS, E1])
        pr = sb("pr", [P, TPS, E1])
        ahead = sb("ahead", [P, TPS, E1, E1])
        rank = sb("rank", [P, TPS, E1])
        rm = sb("rm", [P, TPS])
        rs = sb("rs", [P, TPS])
        score = sb("score", [P, TPS, E1])
        den = sb("den", [P, TPS])
        s1 = sb("s1", [P, TPS, P])
        sg1 = sb("sg1", [P, RING, 2 * P])
        h1 = sb("h1", [P, RING, 2 * P])
        h1T = sb("h1T", [P, 2, 2 * P])
        gf = sb("gf", [P, 2, P])
        of = sb("of", [P, 2, P])
        xo = sb("xo", [P, 2, P])

        def in_one_place(earlier, last):
            old = []
            for buffers in earlier:
                with ExitStack() as place:
                    old += [place.enter_context(nc.sbuf_tensor(*b)) for b in buffers]
            return old + [sb(*b) for b in last]

        w0_raw, w0_rest = in_one_place([[("w0_raw", [P, GROUPS * 2 * GU0], F32)]], [("w0_rest", [P, GROUPS * 2 * GU0], F32R)])
        xnb0, at, w0_round = in_one_place(
            [[("xnb0", [P, HT, P], F32)], [("at", [P, TPS, SEQ], F32)]], [("w0_round", [P, GROUPS * 2 * GU0], F32R)])
        xnb = (xnb0, sT[:, 0:HT, :])
        w13_raw, w13_rest = in_one_place([[("w13_raw", [P, W13], F32)]], [("w13_rest", [P, W13], F32R)])
        sg0, xc_round, xc_rest = in_one_place(
            [[("sg0", [P, 2, 512], F32)]], [("xc_round", [P, TPS, P], F32R), ("xc_rest", [P, TPS, P], F32R)])
        w13_round, lgT, td, scan = in_one_place(
            [[("w13_round", [P, W13], F32R)]],
            [("lgT", [NR, 2, SEQ], F32), ("td", [P, 2, SEQ], F32), ("scan", [P, 2, SEQ], F32)])

        names = """dummy_set warm consts_in attn0_in attn1_in experts0_in down0_in experts1_in zeroed zero_tile pool_const
            chain vars rstds normed turned xnT_ready routed lgT_ready lg_turned scored rows_ready
            counted placed tot_out slots_ready group_ready bias0_ready bias1_ready
            rec_mm rec_act rec_x rec_scan rec_turned rec_out fused fused_out
            w0_rounded w0_split f_row f_turned f_w f_xT f_xr f_gate f_up f_sg f_h f_hT f_hTs f_down f_y gathered
            c_chain c_gy c_var c_rstd c_xn c_turned c_xT c_round c_copy w13_split c_q c_k c_relu c_expq c_qkT
            c_v c_lg c_lgm c_exp c_scores c_a c_at c_num c_den c_s1
            m_gu m_sg m_h m_hT m_hTs m_y m_gf m_of m_xo""".split()
        s = {n: sem(n) for n in names}
        x_in = [sem(f"x_in{q}") for q in range(SEQS)]
        sorted_in = [sem(f"sorted_in{h}") for h in range(HALVES)]
        y_stored = [sem(f"y_stored{h}") for h in range(HALVES)]
        o_stored = [sem(f"o_stored{i}") for i in range(2)]

        def wait(eng, name, value):
            if not (isinstance(value, int) and value <= 0):
                eng.wait_ge(s[name] if isinstance(name, str) else name, value)

        FREE = 16
        scattered = [sem(f"scattered{h}") for h in range(HALVES)]

        def tile_of(tiles, n):
            return tiles[bass.ds(n, 1)].rearrange("o p c -> (o p) c")

        def seq_of(tiles, q):
            return tiles[:, bass.ds(q * TPS, TPS), :]

        def tile_at(tiles, n):
            return tiles[:, bass.ds(n, 1), :].rearrange("p o c -> p (o c)")

        def before_in_ring(j, u):
            if u >= RING:
                return USEQ * j + u - RING + 1
            if isinstance(j, int) and j == 0:
                return 0
            return USEQ * (j - 1) + max(v for v in range(USEQ) if v % RING == u) + 1

        block = ctx.enter_context(nc.Block())

        @block.sync
        def _(sp):
            for q in range(SEQS):
                sp.dma_start(xa[:, TPS * q:TPS * (q + 1), :], x_t[q]).then_inc(x_in[q], 16)
                if q == 0:
                    sp.dma_start(cst[:, :], consts).then_inc(s["consts_in"], 16)
                    sp.dma_start(r0[:, :], router0).then_inc(s["consts_in"], 16)
            sp.dma_start(a0w[:, :], attn0_w).then_inc(s["attn0_in"], 16)
            sp.dma_start(a0b[:, :], attn0_b).then_inc(s["attn0_in"], 16)
            sp.wait_ge(s["zero_tile"], 1)
            sp.dma_start(sorted_rows.rearrange("(p n r) c -> p n (r c)", p=P, r=2),
                         zero_rows[:, :].unsqueeze(1).broadcast_to([P, SORTED // 2, 2 * ROW])).then_inc(s["zeroed"], 16)
            for to, src in ((a1w, attn1_w), (a1b, attn1_b), (wo, wo1), (bo, bo1)):
                sp.dma_start(to[:, :], src).then_inc(s["attn1_in"], 16)
            sp.dma_start(w0_raw[:, :], gate_up0).then_inc(s["experts0_in"], 16)
            sp.dma_start(w0d[:, :], down0).then_inc(s["down0_in"], 16)
            sp.dma_start(vg_w[:, P:P + E1], w13[:, (2 * E1 + 2) * P:]).then_inc(s["experts1_in"], 16)
            sp.dma_start(w13_raw[:, :], w13[:, 0:W13]).then_inc(s["experts1_in"], 16)
            sp.dma_start(w13_shared[:, :], w13[:, W13:W13 + 2 * P]).then_inc(s["experts1_in"], 16)
            sp.dma_start(w2s[:, :], w2).then_inc(s["experts1_in"], 16)

            for h in range(HALVES):
                sp.wait_ge(scattered[h], 16 * HT)
                n = slice(FT * h, FT * (h + 1))
                sp.dma_start(sorted_sb[:, n, :], rows_t[:, n, :]).then_inc(sorted_in[h], 16)
            for h in range(HALVES):
                sp.wait_ge(s["f_y"], FT * (h + 1))
                n = slice(FT * h, FT * (h + 1))
                sp.dma_start(y_t[:, n, :], sorted_sb[:, n, 0:P]).then_inc(y_stored[h], 16)

            with sp.Fori(0, SEQS) as b:
                for t in range(TPS):
                    sp.wait_ge(s["m_xo"], b * TPS + t + 1)
                    sp.dma_start(tile_of(out_t, b * TPS + t), xo[:, t % 2, :]).then_inc(o_stored[t % 2], 16)
            for par in range(2):
                sp.wait_ge(o_stored[par], FREE + 16 * TILES // 2)
            for h in range(HALVES):
                sp.wait_ge(y_stored[h], 16)

        @block.gpsimd
        def _(pool):
            pool.memset(minus_half[:, :], -0.5).then_inc(s["pool_const"], 1)
            pool.memset(zero_rows[:, :], 0.0).then_inc(s["zero_tile"], 1)
            pool.memset(vo[:, :, P:P + 1], 1.0).then_inc(s["pool_const"], 1)
            pool.wait_ge(s["pool_const"], 2)

            for q in range(SEQS):
                pool.wait_ge(s["vars"], q + 1)
                part = slice(q * TPS, (q + 1) * TPS)
                pool.tensor_tensor(rstd[:, part], var[:, part], minus_half[:, :], ALU.pow).then_inc(s["rstds"], 1)

            pool.wait_ge(s["zeroed"], 16)

            def scatter(tiles):
                for t in tiles:
                    pool.indirect_dma_start(
                        sorted_rows, bass.IndirectOffsetOnAxis(ap=slot[:, t:t + 1], axis=0),
                        rows[:, t, :], None).then_inc(scattered[t // HT], 16)

            pool.wait_ge(s["slots_ready"], 1)
            pool.wait_ge(s["rows_ready"], HSEQ)
            scatter(range(HT))
            for g in range(GROUPS):
                pool.wait_ge(s["w0_rounded"], g + 1)
                c = slice(2 * GU0 * g, 2 * GU0 * (g + 1))
                pool.tensor_tensor(w0_rest[:, c], w0_raw[:, c], w0_round[:, c].bitcast(F32),
                                   ALU.subtract).then_inc(s["w0_split"], 1)

            def gather(b):
                if b % HSEQ == 0:
                    pool.wait_ge(y_stored[b // HSEQ], 16)
                if b > 0:
                    pool.wait_ge(s["gathered"], 16 * TPS * b)
                for t in range(TPS * b, TPS * (b + 1)):
                    pool.indirect_dma_start(
                        ya[:, t, :], None, sorted_y[0:FT * P * (b // HSEQ + 1)],
                        bass.IndirectOffsetOnAxis(ap=slot[:, t:t + 1], axis=0)).then_inc(s["gathered"], 16)

            def row_at_hand(n, par):
                wait(pool, "f_turned", n - 1)
                wait(pool, "f_w", n - 1)
                pool.tensor_copy(srow[:, par, :], tile_at(sorted_sb, n)).then_inc(s["f_row"], 1)

            def rows_at_hand(i):
                for par in range(2):
                    row_at_hand(2 * i + par, par)

            mid = FT // 2
            pool.wait_ge(sorted_in[0], 16)
            rows_at_hand(0)
            pool.wait_ge(s["slots_ready"], HALVES)
            pool.wait_ge(s["rows_ready"], SEQS)
            for i in range(4):
                scatter(range(HT + HT // 4 * i, HT + HT // 4 * (i + 1)))
                rows_at_hand(i + 1)
            with pool.Fori(5, mid) as i:
                rows_at_hand(i)
            pool.wait_ge(sorted_in[1], 16)
            late = SORTED // 2 - HSEQ
            with pool.Fori(mid, late - PAIRS) as i:
                rows_at_hand(i)
            pool.wait_ge(s["rec_turned"], SEQS)
            pool.wait_ge(s["rec_scan"], SEQS)
            pool.wait_ge(s["experts1_in"], 16 * 4)
            for p in range(PAIRS):
                c = slice(4 * P * p, 4 * P * (p + 1))
                rows_at_hand(late - PAIRS + p)
                pool.tensor_copy(w13_round[:, c], w13_raw[:, c]).then_inc(s["w13_split"], 1)
                pool.wait_ge(s["w13_split"], 2 * p + 1)
                pool.tensor_tensor(w13_rest[:, c], w13_raw[:, c], w13_round[:, c].bitcast(F32),
                                   ALU.subtract).then_inc(s["w13_split"], 1)
            for b in range(HSEQ):
                rows_at_hand(late + b)
                gather(b)
            for b in range(SEQS):
                pool.wait_ge(s["c_var"], b + 1)
                pool.tensor_tensor(rstd1[:, :], var1[:, :], minus_half[:, 0:TPS], ALU.pow).then_inc(s["c_rstd"], 1)
                pool.wait_ge(s["c_xT"], b + 1)
                for t in range(TPS):
                    if t == 2:
                        pool.wait_ge(s["c_expq"], b + 1)
                        if b > 0:
                            pool.wait_ge(s["c_a"], TPS * b)
                        for i, to in enumerate((qT, kT)):
                            pool.tensor_tensor(to[:, :], relu_qk[:, i, :], exp_qk[:, i, :], ALU.add).then_inc(s["c_qkT"], 1)
                        if HSEQ + b < SEQS:
                            gather(HSEQ + b)
                    if b > 0:
                        pool.wait_ge(s["m_gu"], USEQ * (b - 1) + UNITS * (t + 1))
                    pool.tensor_copy(xc_round[:, t, :], xn1T[:, t * P:(t + 1) * P]).then_inc(s["c_round"], 1)
                    pool.tensor_copy(xc[:, t, :], xn1T[:, t * P:(t + 1) * P])
                    pool.wait_ge(s["c_round"], TPS * b + t + 1)
                    pool.tensor_tensor(xc_rest[:, t, :], xn1T[:, t * P:(t + 1) * P], xc_round[:, t, :].bitcast(F32),
                                       ALU.subtract).then_inc(s["c_copy"], 1)

        @block.scalar
        def _(act):
            act.wait_ge(s["dummy_set"], 1)
            nc.scalar.activation(dummy[:, 1:2], dummy[:, 0:1], ACT.Silu).then_inc(s["warm"], 1)

            def xnT_out(h, j):
                act.wait_ge(s["turned"], HSEQ * h + j + 1)
                q = HSEQ * h + j
                nc.scalar.copy(xnT[:, q * SEQ:(q + 1) * SEQ], ps[:, j, :]).then_inc(s["xnT_ready"], 1)

            def lgT_out(h, j):
                act.wait_ge(s["routed"], HSEQ * h + j + 1)
                if HSEQ * h + j >= 2:
                    act.wait_ge(s["lg_turned"], HSEQ * h + j - 1)
                nc.scalar.copy(lgT[:, j % 2, :], ps[0:NR, 4 + j % 2, :]).then_inc(s["lgT_ready"], 1)

            for h in range(HALVES):
                xnT_out(h, 0)
                xnT_out(h, 1)
                lgT_out(h, 0)
                lgT_out(h, 1)
                xnT_out(h, 2)
                xnT_out(h, 3)
                lgT_out(h, 2)
                lgT_out(h, 3)
                act.wait_ge(s["lg_turned"], HSEQ * (h + 1))
                nc.scalar.activation(th_r[:, :, :], ps[:, 6, 0:HT * NR].rearrange("p (t r) -> p t r", r=NR),
                                     ACT.Tanh, scale=0.5).then_inc(s["scored"], 1)
                for j in range(HSEQ):
                    t = HT * h + TPS * j
                    nc.scalar.copy(rows[:, t:t + TPS, 0:P], xnb[h][:, TPS * j:TPS * (j + 1), :]).then_inc(s["rows_ready"], 1)

            act.wait_ge(s["bias0_ready"], 1)

            def rec_tanh(q, par):
                act.wait_ge(s["rec_mm"], q + 1)
                wait(act, "rec_scan", q - 1)
                nc.scalar.activation(tg[:, par, :], ps[:, 3 * par, :], ACT.Tanh, bias=a0bh[:, 0:1], scale=0.5)
                nc.scalar.activation(tv[:, par, :], ps[:, 3 * par + 1, :], ACT.Tanh, bias=a0b[:, 1:2])
                nc.scalar.activation(td[:, par, :], ps[:, 3 * par + 2, :], ACT.Tanh, bias=a0bh[:, 2:3],
                                     scale=0.5).then_inc(s["rec_act"], 1)

            def rec_out(q, par):
                act.wait_ge(s["rec_turned"], q + 1)
                nc.scalar.copy(seq_of(sT, q), ps[:, 6 + par, :].rearrange("p (t d) -> p t d", d=P)).then_inc(s["rec_out"], 1)

            def round_w0(g):
                c = slice(2 * GU0 * g, 2 * GU0 * (g + 1))
                nc.scalar.copy(w0_round[:, c], w0_raw[:, c]).then_inc(s["w0_rounded"], 1)

            def rec_pair(i):
                for par in range(2):
                    rec_tanh(2 * i + par, par)
                    rec_out(2 * i + par - 2, par)

            act.wait_ge(s["experts0_in"], 16)
            act.wait_ge(s["rows_ready"], HSEQ)
            round_w0(0)
            rec_tanh(0, 0)
            round_w0(1)
            rec_tanh(1, 1)
            round_w0(2)
            round_w0(3)
            act.wait_ge(s["rows_ready"], SEQS)
            with act.Fori(1, SEQS // 2) as i:
                rec_pair(i)
            def sxT_out(n, par):
                act.wait_ge(s["f_turned"], n + 1)
                nc.scalar.copy(sx_round[:, par, :], ps[:, 7, 0:P]).then_inc(s["f_xT"], 1)

            def gate_silu(n, par):
                act.wait_ge(s["f_gate"], n + 1)
                wait(act, "f_h", n - 1)
                nc.scalar.activation(sg0[:, par, :], ps[:, par, :], ACT.Silu).then_inc(s["f_sg"], 1)

            def h0T_out(n, par):
                act.wait_ge(s["f_hT"], n + 1)
                nc.scalar.copy(h0T[:, par, :], ps[:, 4 + par, :]).then_inc(s["f_hTs"], 1)

            def experts0_slot(n, par, before=1, after=1):
                gate_silu(n, par)
                if after:
                    sxT_out(n + 1, 1 - par)
                if before:
                    h0T_out(n - 1, 1 - par)

            def front(k, u):
                if u == 0:
                    act.wait_ge(s["gathered"], 16 * TPS * (k + 1))
                    nc.scalar.activation(gy[:, :].rearrange("p (t d) -> p t d", d=P), seq_of(ya, k),
                                         ACT.Silu).then_inc(s["c_gy"], 1)
                if u == 8:
                    act.wait_ge(s["c_turned"], k + 1)
                    wait(act, "c_copy", TPS * k)
                    nc.scalar.copy(xn1T[:, :], ps[:, 4, :]).then_inc(s["c_xT"], 1)
                for at_u, i, name in ((9, 0, "c_q"), (10, 1, "c_k")):
                    if u == at_u:
                        act.wait_ge(s[name], k + 1)
                        wait(act, "c_qkT", 2 * k)
                        nc.scalar.activation(relu_qk[:, i, :], ps[:, 5 + i, :], ACT.Relu, bias=a1b[:, i:i + 1])
                        nc.scalar.activation(exp_qk[:, i, :], ps[:, 5 + i, :], ACT.Relu, bias=a1bn[:, i:i + 1],
                                             scale=-1.0).then_inc(s["c_relu"], 1)
                if u == EXP_AT:
                    act.wait_ge(s["c_relu"], 2 * (k + 1))
                    nc.scalar.activation(exp_qk[:, :, :], exp_qk[:, :, :], ACT.Exp, scale=-1.0).then_inc(s["c_expq"], 1)
                    act.wait_ge(s["c_lgm"], k + 1)
                    nc.scalar.activation(e1[:, :, :], lg[:, :, :], ACT.Exp).then_inc(s["c_exp"], 1)

            sxT_out(0, 0)
            rec_out(SEQS - 2, 0)
            rec_out(SEQS - 1, 1)
            experts0_slot(0, 0, before=0)
            experts0_slot(1, 1)
            with act.Fori(1, SORTED // 2 - 1) as i:
                experts0_slot(2 * i, 0)
                experts0_slot(2 * i + 1, 1)
            experts0_slot(SORTED - 2, 0)
            front(0, 0)
            experts0_slot(SORTED - 1, 1, after=0)
            h0T_out(SORTED - 1, 1)

            def unit_silu(j, u):
                t, p = divmod(u, UNITS)
                n = USEQ * j + u
                if u == 0:
                    act.wait_ge(s["c_scores"], j + 1)
                act.wait_ge(s["m_gu"], n + 1)
                wait(act, "m_h", before_in_ring(j, u))
                bank = ps[:, BANKS[u % RING], :]
                if p < PAIRS:
                    for e in range(2):
                        last = nc.scalar.activation(sg1[:, u % RING, e * P:(e + 1) * P], bank[:, e * P:(e + 1) * P],
                                                    ACT.Silu, scale=score[:, t, 2 * p + e:2 * p + e + 1])
                else:
                    last = nc.scalar.activation(sg1[:, u % RING, 0:P], bank[:, 0:P], ACT.Silu)
                last.then_inc(s["m_sg"], 1)

            def unit_hT(j, u):
                n = USEQ * j + u
                w = 2 * P if u % UNITS < PAIRS else P
                act.wait_ge(s["m_hT"], n + 1)
                if u - 1 in DVE_TURNS:
                    act.wait_ge(s["m_hTs"], n)
                nc.scalar.copy(h1T[:, u % 2, 0:w], ps[:, 2, 0:w]).then_inc(s["m_hTs"], 1)

            def final_silu(j, t):
                act.wait_ge(s["m_y"], USEQ * j + UNITS * (t + 1))
                if t >= 2:
                    act.wait_ge(s["m_of"], TPS * j + t - 1)
                else:
                    wait(act, "m_of", TPS * j + t - 1)
                nc.scalar.activation(gf[:, t % 2, :], ps[:, 3, 0:P], ACT.Silu).then_inc(s["m_gf"], 1)

            def step(k, fronts=True, tiles=True, before=True, start=0):
                for u in range(start, USEQ):
                    if tiles:
                        unit_silu(k - 1, u)
                        if (before or u >= 2) and u - 2 not in DVE_TURNS:
                            unit_hT(k - 1, u - 2)
                        if (u - 2) % UNITS == 0 and (before or u > 2):
                            final_silu(k - 1, (u - 2) // UNITS - 1)
                    if fronts:
                        front(k, u)

            act.wait_ge(s["bias1_ready"], 1)
            step(0, tiles=False, start=1)
            step(1, before=False)
            with act.Fori(2, SEQS) as k:
                step(k)
            step(SEQS, fronts=False)
            unit_hT(SEQS - 1, USEQ - 2)
            unit_hT(SEQS - 1, USEQ - 1)
            final_silu(SEQS - 1, TPS - 1)

        @block.tensor
        def _(pe):
            pe.wait_ge(s["consts_in"], 32)

            def turn_xn(h, j):
                pe.wait_ge(s["normed"], HSEQ * h + j + 1)
                for t in range(TPS):
                    last = pe.transpose(ps[:, j, t * P:(t + 1) * P], xnb[h][:, TPS * j + t, :], ident)
                last.then_inc(s["turned"], 1)

            def route(h, j):
                q = HSEQ * h + j
                pe.wait_ge(s["xnT_ready"], q + 1)
                if q >= 2:
                    pe.wait_ge(s["lgT_ready"], q - 1)
                pe.matmul(ps[0:NR, 4 + j % 2, :], r0[:, :], xnT[:, q * SEQ:(q + 1) * SEQ],
                          start=True, stop=True).then_inc(s["routed"], 1)

            def turn_logits(h, j):
                pe.wait_ge(s["lgT_ready"], HSEQ * h + j + 1)
                if h > 0 and j == 0:
                    pe.wait_ge(s["scored"], h)
                for t in range(TPS):
                    c = (TPS * j + t) * NR
                    last = pe.transpose(ps[:, 6, c:c + NR], lgT[:, j % 2, t * P:(t + 1) * P], ident[0:NR, 0:NR])
                last.then_inc(s["lg_turned"], 1)

            def place(h):
                pe.wait_ge(s["counted"], h + 1)
                pe.matmul(ps[:, 7, 0:GROUPS], lower, cum[:, :, HT - 1], start=True, stop=True)
                pe.matmul(ps[:, 7, GROUPS:2 * GROUPS], ones, cum[:, :, HT - 1], start=True, stop=True).then_inc(s["placed"], 1)

            for h in range(HALVES):
                if h == 0:
                    turn_xn(h, 0)
                    turn_xn(h, 1)
                route(h, 0)
                route(h, 1)
                turn_xn(h, 2)
                turn_xn(h, 3)
                if h == 1:
                    place(0)
                turn_logits(h, 0)
                turn_logits(h, 1)
                route(h, 2)
                route(h, 3)
                turn_logits(h, 2)
                turn_logits(h, 3)
                if h == 0:
                    turn_xn(1, 0)
                    turn_xn(1, 1)

            pe.wait_ge(s["attn0_in"], 32)

            def rec_project(q, par):
                wait(pe, "rec_act", q - 1)
                for i in range(3):
                    last = pe.matmul(ps[:, 3 * par + i, :], a0w[:, i * P:(i + 1) * P],
                                     xnT[:, bass.ds(q * SEQ, SEQ)], start=True, stop=True)
                last.then_inc(s["rec_mm"], 1)

            def rec_turn(q, par):
                pe.wait_ge(s["rec_scan"], q + 1)
                pe.wait_ge(s["rec_out"], FREE + q - 1)
                for t in range(TPS):
                    last = pe.transpose(ps[:, 6 + par, t * P:(t + 1) * P], scan[:, par, t * P:(t + 1) * P], ident)
                last.then_inc(s["rec_turned"], 1)

            rec_project(0, 0)
            pe.wait_ge(s["scored"], HALVES)
            pe.wait_ge(s["attn1_in"], 16 * 4)
            pe.wait_ge(s["bias1_ready"], 1)
            pe.matmul(ps[:, 6, 0:P], a1w[:, 2 * P:3 * P], wo[:, :], start=True, stop=True)
            pe.matmul(ps[:, 6, P:2 * P], bv_cols[:, :], wo[:, :], start=True, stop=True).then_inc(s["fused"], 1)
            rec_project(1, 1)
            rec_project(2, 0)
            pe.wait_ge(s["fused_out"], 1)
            rec_turn(0, 0)
            rec_project(3, 1)
            place(1)
            pe.wait_ge(s["tot_out"], HALVES)
            rec_turn(1, 1)
            with pe.Fori(2, SEQS // 2) as i:
                for par in range(2):
                    rec_project(2 * i + par, par)
                    rec_turn(2 * i + par - 2, par)
            pe.wait_ge(s["w0_split"], GROUPS)
            pe.wait_ge(s["down0_in"], 16)
            pe.wait_ge(s["group_ready"], HALVES)
            at_hand = [pe.alloc_register(f"at_hand{par}") for par in range(2)]
            behind = [pe.alloc_register(f"behind{par}") for par in range(2)]

            def group_of(reg):
                return pe.snap(reg, min_val=0, max_val=(GROUPS - 1) * D0)

            def turn_rows(n, par):
                pe.wait_ge(s["f_row"], n + 1)
                pe.transpose(ps[:, 7, 0:P], srow[:, par, 0:P], ident).then_inc(s["f_turned"], 1)

            def in_parts(bank, par, c):
                pe.matmul(bank, sx_round[:, par, :], w0_round[:, c], start=True, stop=False)
                pe.matmul(bank, sx_rest[:, par, :], w0_round[:, c], start=False, stop=False)
                return pe.matmul(bank, sx_round[:, par, :], w0_rest[:, c], start=False, stop=True)

            def gate(n, par):
                g = group_of(at_hand[par])
                pe.wait_ge(s["f_xr"], n + 1)
                in_parts(ps[:, par, :], par, bass.ds(g * (2 * GU0 // D0), GU0)).then_inc(s["f_gate"], 1)

            def up(n, par):
                g = group_of(at_hand[par])
                in_parts(ps[:, 2 + par, :], par, bass.ds(g * (2 * GU0 // D0) + GU0, GU0)).then_inc(s["f_up"], 1)

            def turn_h0(n, par):
                pe.wait_ge(s["f_h"], n + 1)
                for c in range(HC):
                    last = pe.transpose(ps[:, 4 + par, c * P:(c + 1) * P], h0[:, par, c * P:(c + 1) * P], ident)
                last.then_inc(s["f_hT"], 1)

            def down(n, par):
                g = group_of(behind[par])
                pe.wait_ge(s["f_hTs"], n + 1)
                wait(pe, "f_y", n)
                for c in range(HC):
                    last = pe.matmul(ps[:, 6, 0:P], h0T[:, par, c * P:(c + 1) * P],
                                     w0d[:, bass.ds(g + c * P, P)], start=(c == 0), stop=(c == HC - 1))
                last.then_inc(s["f_down"], 1)

            def experts0_slot(n, par, before=2, after=1):
                gate(n, par)
                if after:
                    turn_rows(n + 1, 1 - par)
                up(n, par)
                if after:
                    pe.reg_load(at_hand[1 - par], group[0:1, bass.ds(n + 1, 1)])
                if before > 1:
                    down(n - 2, par)
                pe.reg_mov(behind[par], at_hand[par])
                if before > 0:
                    turn_h0(n - 1, 1 - par)

            pe.reg_load(at_hand[0], group[0:1, 0:1])
            pe.wait_ge(s["rec_out"], FREE + SEQS - 2)
            turn_rows(0, 0)
            rec_turn(SEQS - 2, 0)
            pe.wait_ge(s["rec_act"], SEQS)
            gate(0, 0)
            rec_turn(SEQS - 1, 1)
            up(0, 0)
            pe.reg_mov(behind[0], at_hand[0])
            pe.reg_load(at_hand[1], group[0:1, 1:2])
            pe.wait_ge(s["rec_out"], FREE + SEQS)
            turn_rows(1, 1)
            experts0_slot(1, 1, before=1)
            with pe.Fori(1, SORTED // 2 - 1) as i:
                experts0_slot(2 * i, 0)
                experts0_slot(2 * i + 1, 1)
            experts0_slot(SORTED - 2, 0)
            experts0_slot(SORTED - 1, 1, after=0)
            down(SORTED - 2, 0)
            turn_h0(SORTED - 1, 1)
            down(SORTED - 1, 1)

            pe.wait_ge(s["experts1_in"], 16 * 4)
            pe.wait_ge(s["w13_split"], 2 * PAIRS)
            pe.wait_ge(s["f_y"], SORTED)

            def front(k, u):
                if u == 8:
                    pe.wait_ge(s["c_xn"], k + 1)
                    for t in range(TPS):
                        last = pe.transpose(ps[:, 4, t * P:(t + 1) * P], xn1[:, t, :], ident)
                    last.then_inc(s["c_turned"], 1)
                if u == 9:
                    pe.wait_ge(s["c_xT"], k + 1)
                    wait(pe, "c_s1", k)
                    pe.matmul(ps[:, 5, :], a1w[:, 0:P], xn1T[:, :], start=True, stop=True).then_inc(s["c_q"], 1)
                if u == 10:
                    pe.matmul(ps[:, 6, :], a1w[:, P:2 * P], xn1T[:, :], start=True, stop=True).then_inc(s["c_k"], 1)
                for at_u, bank, pair in ((11, 4, 0), (12, 5, 1)):
                    if u == at_u:
                        if pair:
                            pe.wait_ge(s["c_relu"], 2 * k + 1)
                        for t in (2 * pair, 2 * pair + 1):
                            o = (t % 2) * (P + E1)
                            last = pe.matmul(ps[:, bank, o:o + P + E1], xn1T[:, t * P:(t + 1) * P], vg_w[:, :],
                                             start=True, stop=True)
                        last.then_inc(s["c_v"], 1)

            def scores(k, sr):
                if sr == 0:
                    pe.wait_ge(s["c_qkT"], 2 * (k + 1))
                    pe.wait_ge(s["c_lg"], 2 * (k + 1))
                if sr == 3:
                    pe.wait_ge(s["c_at"], TPS * k + 1)
                pe.matmul(ps[:, SCORE_BANKS[sr], 0:SEQ - sr * P], kT[:, sr * P:(sr + 1) * P], qT[:, sr * P:SEQ],
                          start=True, stop=True).then_inc(s["c_a"], 1)

            def attend(j):
                pe.wait_ge(s["c_at"], TPS * (j + 1))
                for c in range(TPS):
                    o = (c % 2) * (P + 1)
                    for sr in range(c + 1):
                        last = pe.matmul(ps[:, 5 + c // 2, o:o + P + 1], at[:, sr, c * P:(c + 1) * P], vo[:, sr, :],
                                         start=(sr == 0), stop=(sr == c))
                last.then_inc(s["c_num"], 1)

            def unit_gu(j, u):
                t, p = divmod(u, UNITS)
                w = 4 * P if p < PAIRS else 2 * P
                if p == 0:
                    pe.wait_ge(s["c_copy"], TPS * j + t + 1)
                wait(pe, "m_h", before_in_ring(j, u))
                bank = ps[:, BANKS[u % RING], 0:w]
                c = slice(4 * P * p, 4 * P * p + w)
                if p < PAIRS:
                    pe.matmul(bank, xc_round[:, t, :], w13_round[:, c], start=True, stop=False)
                    pe.matmul(bank, xc_round[:, t, :], w13_rest[:, c], start=False, stop=False)
                    last = pe.matmul(bank, xc_rest[:, t, :], w13_round[:, c], start=False, stop=True)
                else:
                    last = pe.matmul(bank, xc[:, t, :], w13_shared[:, :], start=True, stop=True)
                last.then_inc(s["m_gu"], 1)

            def unit_turn(j, u):
                n = USEQ * j + u
                pe.wait_ge(s["m_h"], n + 1)
                wait(pe, "m_hTs", n)
                for e in range(2 if u % UNITS < PAIRS else 1):
                    last = pe.transpose(ps[:, 2, e * P:(e + 1) * P], h1[:, u % USEQ % RING, e * P:(e + 1) * P], ident)
                last.then_inc(s["m_hT"], 1)

            def unit_down(j, u):
                t, p = divmod(u, UNITS)
                n = USEQ * j + u
                pe.wait_ge(s["m_hTs"], n + 1)
                if p == 0:
                    pe.wait_ge(s["m_gf"], FREE + TPS * j + t)
                for e in range(2 if p < PAIRS else 1):
                    last = pe.matmul(ps[:, 3, 0:P], h1T[:, u % 2, e * P:(e + 1) * P],
                                     w2s[:, (2 * p + e) * P:(2 * p + e + 1) * P],
                                     start=(p == 0 and e == 0), stop=(p == PAIRS))
                last.then_inc(s["m_y"], 1)

            def step(k, fronts=True, tiles=True, before=True):
                for u in range(USEQ):
                    if tiles:
                        unit_gu(k - 1, u)
                        if before or u >= 2:
                            unit_turn(k - 1, u - 2)
                        if 1 <= u <= TPS:
                            scores(k - 1, u - 1)
                        if before or u >= 3:
                            unit_down(k - 1, u - 3)
                        if u == TPS + 2:
                            attend(k - 1)
                    if fronts:
                        front(k, u)

            step(0, tiles=False)
            step(1, before=False)
            with pe.Fori(2, SEQS) as k:
                step(k)
            step(SEQS, fronts=False)
            unit_turn(SEQS - 1, USEQ - 2)
            unit_down(SEQS - 1, USEQ - 3)
            unit_turn(SEQS - 1, USEQ - 1)
            unit_down(SEQS - 1, USEQ - 2)
            unit_down(SEQS - 1, USEQ - 1)

        @block.vector
        def _(dve):
            chain = [0]

            def link(ins):
                chain[0] += 1
                ins.then_inc(s["chain"], 1)
                dve.wait_ge(s["chain"], chain[0])

            nc.vector.memset(dummy[:, :], 0.0).then_inc(s["dummy_set"], 1)
            dve.sem_inc(s["rec_out"], FREE)
            dve.sem_inc(s["m_gf"], FREE)
            for par in range(2):
                dve.sem_inc(o_stored[par], FREE)

            def stats(q):
                tiles = range(TPS * q, TPS * (q + 1))
                dve.wait_ge(x_in[q], 16)
                for t in tiles:
                    last = nc.vector.bn_stats(st[:, t, :], xa[:, t, :])
                link(last)
                for t in tiles:
                    last = nc.vector.bn_aggr(mv[:, t, :], st[:, t, :])
                link(last)
                nc.vector.tensor_scalar(var[:, tiles.start:tiles.stop], mv[:, tiles.start:tiles.stop, 1], LN_EPS, None,
                                        ALU.add).then_inc(s["vars"], 1)

            def normalise(q):
                dve.wait_ge(s["rstds"], q + 1)
                for t in range(TPS * q, TPS * (q + 1)):
                    last = nc.vector.tensor_scalar(xnb[t // HT][:, t % HT, :], xa[:, t, :], mv[:, t, 0:1], rstd[:, t:t + 1],
                                                   ALU.subtract, ALU.mult)
                last.then_inc(s["normed"], 1)

            macro = sc_r[:, :, 0:GROUPS]
            micro = sc_r[:, :, GROUPS:NR].rearrange("p t (g e) -> p t g e", e=EPG)
            to_groups = [P, HT, GROUPS]

            def groups(h):
                dve.wait_ge(s["scored"], h + 1)
                link(nc.vector.tensor_scalar(sc_r[:, :, :], th_r[:, :, :], 0.5, 0.5, ALU.mult, ALU.add))
                link(nc.vector.tensor_reduce(best[:, :], macro, AX_X, ALU.max))
                link(nc.vector.tensor_tensor(ohg[:, :, :], macro, best[:, :].unsqueeze(2).broadcast_to(to_groups), ALU.is_ge))
                link(nc.vector.tensor_tensor(ohg[:, :, :], ohg[:, :, :],
                                             fall[:, E1 - GROUPS:E1].unsqueeze(1).broadcast_to(to_groups), ALU.mult))
                link(nc.vector.tensor_reduce(best_e[:, :], ohg[:, :, :], AX_X, ALU.max))
                link(nc.vector.tensor_tensor(ohg[:, :, :], ohg[:, :, :],
                                             best_e[:, :].unsqueeze(2).broadcast_to(to_groups), ALU.is_equal))
                if h > 0:
                    dve.wait_ge(s["placed"], h)
                for g in range(GROUPS):
                    last = nc.vector.tensor_tensor_scan(cum[:, g, :], ones[:, 0:HT], ohg[:, :, g], 0.0, ALU.mult, ALU.add)
                last.then_inc(s["counted"], 1)

            def weights_of_groups(h):
                link(nc.vector.tensor_tensor(usum[:, :, :], micro[:, :, :, 0], micro[:, :, :, 1], ALU.add))
                link(nc.vector.tensor_scalar(usum[:, :, :], usum[:, :, :], TOPK_EPS, None, ALU.add))
                link(nc.vector.reciprocal(usum[:, :, :], usum[:, :, :]))
                link(nc.vector.tensor_scalar(mfac[:, :], best[:, :], TOPK_EPS, None, ALU.add))
                link(nc.vector.reciprocal(mfac[:, :], mfac[:, :]))
                link(nc.vector.tensor_tensor(mfac[:, :], mfac[:, :], best[:, :], ALU.mult))
                link(nc.vector.tensor_tensor(usum[:, :, :], usum[:, :, :],
                                             mfac[:, :].unsqueeze(2).broadcast_to(to_groups), ALU.mult))
                link(nc.vector.tensor_tensor(usum[:, :, :], usum[:, :, :], ohg[:, :, :], ALU.mult))
                link(nc.vector.tensor_tensor(uw[:, :, :, :], micro,
                                             usum[:, :, :].unsqueeze(3).broadcast_to([P, HT, GROUPS, EPG]), ALU.mult))
                nc.vector.tensor_reduce(rows[:, HT * h:HT * (h + 1), P:ROW], uw[:, :, :, :].rearrange("p t g e -> p t e g"),
                                        AX_X, ALU.add)

            def counts(h):
                dve.wait_ge(s["placed"], h + 1)
                nc.vector.tensor_copy(tot[:, :], ps[:, 7, 0:2 * GROUPS]).then_inc(s["tot_out"], 1)

            def slots(h):
                dve.wait_ge(s["tot_out"], h + 1)
                link(nc.vector.tensor_scalar(ntile[:, :], tot[:, GROUPS:2 * GROUPS], 1.0 / P, (P / 2 - 0.5) / P,
                                             ALU.mult, ALU.add))
                link(nc.vector.tensor_scalar(ntile[:, :], ntile[:, :], MAGIC, MAGIC, ALU.add, ALU.subtract))
                link(nc.vector.tensor_tensor_scan(ends[:, :], ones[:, 0:GROUPS], ntile[:, :], 0.0, ALU.mult, ALU.add))
                link(nc.vector.tensor_tensor(base[:, :], ends[:, :], ntile[:, :], ALU.subtract))
                link(nc.vector.scalar_tensor_tensor(base[:, :], base[:, :], float(P), tot[:, 0:GROUPS], ALU.mult, ALU.add))
                link(nc.vector.tensor_scalar(base[:, :], base[:, :], float(h * FT * P - 1), None, ALU.add))
                link(nc.vector.tensor_tensor(where[:, :, :], cum[:, :, :],
                                             base[:, :].unsqueeze(2).broadcast_to([P, GROUPS, HT]), ALU.add))
                link(nc.vector.tensor_tensor(where[:, :, :], where[:, :, :], ohg[:, :, :].rearrange("p t g -> p g t"), ALU.mult))
                link(nc.vector.tensor_reduce(slot_f[:, :], where[:, :, :].rearrange("p g t -> p t g"), AX_X, ALU.add))
                nc.vector.tensor_copy(slot[:, HT * h:HT * (h + 1)], slot_f[:, :]).then_inc(s["slots_ready"], 1)
                link(nc.vector.tensor_tensor(past[0:1, :, :],
                                             cst[0:1, C_TILE:C_TILE + FT].unsqueeze(2).broadcast_to([1, FT, GROUPS - 1]),
                                             ends[0:1, 0:GROUPS - 1].unsqueeze(1).broadcast_to([1, FT, GROUPS - 1]), ALU.is_ge))
                link(nc.vector.tensor_reduce(group_f[:, :], past[0:1, :, :], AX_X, ALU.add))
                link(nc.vector.tensor_scalar(group_f[:, :], group_f[:, :], float(D0), None, ALU.mult))
                nc.vector.tensor_copy(group[:, FT * h:FT * (h + 1)], group_f[:, :]).then_inc(s["group_ready"], 1)

            stats(0)
            for q in range(1, SEQS):
                stats(q)
                normalise(q - 1)
            normalise(SEQS - 1)
            dve.wait_ge(s["consts_in"], 32)
            groups(0)
            weights_of_groups(0)
            counts(0)
            slots(0)
            dve.wait_ge(s["attn0_in"], 32)
            nc.vector.tensor_scalar(a0bh[:, :], a0b[:, :], 0.5, None, ALU.mult).then_inc(s["bias0_ready"], 1)
            dve.wait_ge(s["attn1_in"], 16 * 4)
            nc.vector.tensor_scalar(a1bn[:, :], a1b[:, 0:2], -1.0, None, ALU.mult)
            nc.vector.tensor_scalar(bv_cols[:, :], ones, a1b[:, 2:3], None, ALU.mult).then_inc(s["bias1_ready"], 1)

            def rec_scan(q, par):
                dve.wait_ge(s["rec_act"], q + 1)
                nc.vector.tensor_scalar(td[:, par, :], td[:, par, :], 0.499, 0.5, ALU.mult, ALU.add).then_inc(s["rec_x"], 1)
                nc.vector.scalar_tensor_tensor(tg[:, par, :], tg[:, par, :], 1.0, tv[:, par, :],
                                               ALU.add, ALU.mult).then_inc(s["rec_x"], 1)
                dve.wait_ge(s["rec_x"], 2 * q + 2)
                wait(dve, "rec_turned", q - 1)
                nc.vector.tensor_tensor_scan(scan[:, par, :], td[:, par, :], tg[:, par, :], 0.0,
                                             ALU.mult, ALU.add).then_inc(s["rec_scan"], 1)

            dve.wait_ge(s["fused"], 1)
            nc.vector.tensor_copy(vg_w[:, 0:P], ps[:, 6, 0:P])
            nc.vector.tensor_copy(bv_wo[:, :], ps[:, 6, P:2 * P]).then_inc(s["fused_out"], 1)

            rec_scan(0, 0)
            rec_scan(1, 1)
            groups(1)
            counts(1)
            rec_scan(2, 0)
            weights_of_groups(1)
            slots(1)
            rec_scan(3, 1)
            with dve.Fori(2, SEQS // 2) as i:
                rec_scan(2 * i, 0)
                rec_scan(2 * i + 1, 1)


            def weights(n, par):
                dve.wait_ge(s["f_row"], n + 1)
                wait(dve, "f_h", n - 1)
                nc.vector.tensor_copy(sw[:, par, :], srow[:, par, P:ROW]).then_inc(s["f_w"], 1)

            def rest_of_rows(n, par):
                dve.wait_ge(s["f_xT"], n + 1)
                nc.vector.tensor_tensor(sx_rest[:, par, :], ps[:, 7, 0:P], sx_round[:, par, :].bitcast(F32),
                                        ALU.subtract).then_inc(s["f_xr"], 1)

            def hidden(n, par):
                dve.wait_ge(s["f_sg"], n + 1)
                wait(dve, "f_hT", n - 1)
                dve.wait_ge(s["f_w"], n + 1)
                dve.wait_ge(s["f_up"], n + 1)
                for e in range(EPG):
                    c = slice(e * F0, (e + 1) * F0)
                    last = nc.vector.scalar_tensor_tensor(h0[:, par, c], sg0[:, par, c], sw[:, par, e:e + 1],
                                                          ps[:, 2 + par, c], ALU.mult, ALU.mult)
                last.then_inc(s["f_h"], 1)

            def result(n):
                dve.wait_ge(s["f_down"], n + 1)
                nc.vector.tensor_copy(tile_at(sorted_sb, n)[:, 0:P], ps[:, 6, 0:P]).then_inc(s["f_y"], 1)

            def experts0_slot(n, par, before=2, after=1):
                if after:
                    weights(n + 1, 1 - par)
                    rest_of_rows(n + 1, 1 - par)
                if before > 1:
                    result(n - 2)
                hidden(n, par)

            R_AT = (1, 1, 1, 1, 0, 0, 0, 0, 0, 0, 0, 0, 1, 3, 0, 2, 0, 1, 0, 0)
            R_STEPS = sum(R_AT)

            def front(k, u):
                n = [R_STEPS * k + sum(R_AT[:u])]

                def then(ins):
                    n[0] = n[0] + 1
                    ins.then_inc(s["c_chain"], 1)
                    dve.wait_ge(s["c_chain"], n[0])

                g3 = gy[:, :].rearrange("p (t d) -> p t d", d=P)
                if u == 0:
                    dve.wait_ge(s["c_gy"], k + 1)
                    then(nc.vector.tensor_tensor(g3, g3, seq_of(sT, k), ALU.mult))
                if u == 1:
                    then(nc.vector.scalar_tensor_tensor(seq_of(xa, k), g3, 0.5, seq_of(xa, k), ALU.mult, ALU.add))
                if u == 2:
                    for t in range(TPS):
                        last = nc.vector.bn_stats(st1[:, t, :], xa[:, bass.ds(k * TPS + t, 1), :].rearrange("p o d -> p (o d)"))
                    then(last)
                if u == 3:
                    for t in range(TPS):
                        last = nc.vector.bn_aggr(mv1[:, t, :], st1[:, t, :])
                    then(last)
                    nc.vector.tensor_scalar(var1[:, :], mv1[:, :, 1], LN_EPS, None, ALU.add).then_inc(s["c_var"], 1)
                if u == 5:
                    dve.wait_ge(s["c_rstd"], k + 1)
                    for t in range(TPS):
                        last = nc.vector.tensor_scalar(xn1[:, t, :], xa[:, bass.ds(k * TPS + t, 1), :].rearrange("p o d -> p (o d)"),
                                                       mv1[:, t, 0:1], rstd1[:, t:t + 1], ALU.subtract, ALU.mult)
                    last.then_inc(s["c_xn"], 1)
                for at_u, bank, pair in ((11, 4, 0), (12, 5, 1)):
                    if u == at_u:
                        dve.wait_ge(s["c_v"], 2 * k + pair + 1)
                        two = ps[:, bank, 0:2 * (P + E1)].rearrange("p (t c) -> p t c", c=P + E1)
                        nc.vector.tensor_tensor(vo[:, 2 * pair:2 * pair + 2, 0:P], two[:, :, 0:P],
                                                bv_wo[:, :].unsqueeze(1).broadcast_to([P, 2, P]), ALU.add)
                        nc.vector.tensor_copy(lg[:, 2 * pair:2 * pair + 2, :], two[:, :, P:P + E1]).then_inc(s["c_lg"], 1)
                if u == 12:
                    dve.wait_ge(s["c_lg"], 2 * (k + 1))
                    then(nc.vector.tensor_reduce(rm[:, :], lg[:, :, :], AX_X, ALU.max))
                    nc.vector.tensor_tensor(lg[:, :, :], lg[:, :, :], rm[:, :].unsqueeze(2).broadcast_to([P, TPS, E1]),
                                            ALU.subtract).then_inc(s["c_lgm"], 1)
                if u == 13:
                    pairs = [P, TPS, E1, E1]
                    dve.wait_ge(s["c_lgm"], k + 1)
                    then(nc.vector.tensor_tensor(ahead[:, :, :, :], lg[:, :, :].unsqueeze(2).broadcast_to(pairs),
                                                 lg[:, :, :].unsqueeze(3).broadcast_to(pairs), ALU.subtract))
                    flat = ahead[:, :, :, :].rearrange("p t e o -> p t (e o)")
                    before = cst[:, C_BEFORE:CONSTS].unsqueeze(1).broadcast_to([P, TPS, E1 * E1])
                    then(nc.vector.tensor_tensor(flat, flat, before, ALU.is_gt))
                    then(nc.vector.tensor_reduce(rank[:, :, :], ahead[:, :, :, :], AX_X, ALU.add))
                if u == 15:
                    dve.wait_ge(s["c_exp"], k + 1)
                    then(nc.vector.tensor_reduce(rs[:, :], e1[:, :, :], AX_X, ALU.add))
                    then(nc.vector.reciprocal(rs[:, :], rs[:, :]))
                if u == 17:
                    then(nc.vector.tensor_tensor(pr[:, :, :], e1[:, :, :], rs[:, :].unsqueeze(2).broadcast_to([P, TPS, E1]),
                                                 ALU.mult))
                if u == 19:
                    wait(dve, "m_h", USEQ * k - 1)
                    nc.vector.scalar_tensor_tensor(score[:, :, :], rank[:, :, :], float(TOPK1), pr[:, :, :],
                                                   ALU.is_lt, ALU.mult).then_inc(s["c_scores"], 1)
                assert not isinstance(k, int) or n[0] == R_STEPS * k + sum(R_AT[:u + 1]), (u, n)

            weights(0, 0)
            rest_of_rows(0, 0)
            experts0_slot(0, 0, before=0)
            experts0_slot(1, 1, before=1)
            with dve.Fori(1, SORTED // 2 - 1) as i:
                experts0_slot(2 * i, 0)
                experts0_slot(2 * i + 1, 1)
            experts0_slot(SORTED - 2, 0)
            front(0, 0)
            front(0, 1)
            experts0_slot(SORTED - 1, 1, after=0)
            front(0, 2)
            front(0, 3)
            result(SORTED - 2)
            result(SORTED - 1)

            def masked(k, sr):
                dve.wait_ge(s["c_a"], TPS * k + sr + 1)
                w = SEQ - sr * P
                nc.vector.tensor_tensor(at[:, sr, sr * P:SEQ], ps[:, SCORE_BANKS[sr], 0:w], cst[:, C_CAUSAL:C_CAUSAL + w],
                                        ALU.mult).then_inc(s["c_at"], 1)

            def attention(j):
                dve.wait_ge(s["c_num"], j + 1)
                for i in range(2):
                    nc.vector.tensor_scalar(den[:, 2 * i:2 * i + 2],
                                            ps[:, 5 + i, 0:2 * (P + 1)].rearrange("p (t c) -> p t c", c=P + 1)[:, :, P],
                                            ATT_EPS, None, ALU.add).then_inc(s["c_den"], 1)
                dve.wait_ge(s["c_den"], 3 * j + 2)
                nc.vector.reciprocal(den[:, :], den[:, :]).then_inc(s["c_den"], 1)
                dve.wait_ge(s["c_den"], 3 * j + 3)
                for c in range(TPS):
                    o = (c % 2) * (P + 1)
                    last = nc.vector.scalar_tensor_tensor(s1[:, c, :], ps[:, 5 + c // 2, o:o + P], den[:, c:c + 1], bo[:, :],
                                                          ALU.mult, ALU.add)
                last.then_inc(s["c_s1"], 1)

            def unit(j, u):
                t, p = divmod(u, UNITS)
                n = USEQ * j + u
                w = 2 * P if p < PAIRS else P
                bank = ps[:, BANKS[u % RING], :]
                dve.wait_ge(s["m_sg"], n + 1)
                wait(dve, "m_hT", before_in_ring(j, u))
                for e in range(w // P):
                    c = slice(e * P, (e + 1) * P)
                    last = nc.vector.scalar_tensor_tensor(
                        h1[:, u % RING, c], sg1[:, u % RING, c], score[:, t, 2 * p + e:2 * p + e + 1] if p < PAIRS else 1.0,
                        bank[:, w + e * P:w + (e + 1) * P], ALU.mult, ALU.mult)
                last.then_inc(s["m_h"], 1)

            def unit_hT(j, u):
                n = USEQ * j + u
                w = 2 * P if u % UNITS < PAIRS else P
                dve.wait_ge(s["m_hT"], n + 1)
                nc.vector.tensor_copy(h1T[:, u % 2, 0:w], ps[:, 2, 0:w]).then_inc(s["m_hTs"], 1)

            def final(j, t):
                par = t % 2
                m = TPS * j + t
                dve.wait_ge(s["m_gf"], FREE + m + 1)
                if t == 0:
                    dve.wait_ge(s["c_s1"], j + 1)
                nc.vector.tensor_tensor(of[:, par, :], gf[:, par, :], s1[:, t % TPS, :], ALU.mult).then_inc(s["m_of"], 1)
                dve.wait_ge(s["m_of"], m + 1)
                dve.wait_ge(o_stored[par], FREE + 16 * (2 * j + t // 2))
                nc.vector.tensor_tensor(xo[:, par, :], of[:, par, :], tile_at(xa, m), ALU.add).then_inc(s["m_xo"], 1)

            def step(k, fronts=True, tiles=True, before=True, start=0):
                for u in range(start, USEQ):
                    if tiles:
                        if u == EXP_AT + 1:
                            for v in DVE_TURNS:
                                unit_hT(k - 1, v)
                        unit(k - 1, u)
                        if 1 <= u <= TPS:
                            masked(k - 1, u - 1)
                        if u == TPS + 3:
                            attention(k - 1)
                        if (u - 2) % UNITS == 0 and (before or u > 2):
                            final(k - 1, (u - 2) // UNITS - 1)
                    if fronts:
                        front(k, u)

            step(0, tiles=False, start=5)
            step(1, before=False)
            with dve.Fori(2, SEQS) as k:
                step(k)
            step(SEQS, fronts=False)
            final(SEQS - 1, TPS - 1)


def kernel(**inputs):
    import numpy as np
    import concourse.bacc as bacc
    from concourse import mybir as mb
    from concourse.bass_utils import run_bass_kernel_spmd

    f = {k: np.asarray(v) for k, v in inputs.items()}
    cat = np.concatenate

    consts = np.zeros((P, CONSTS), np.float32)
    consts[:, C_ID:C_ID + P] = np.eye(P)
    consts[:, C_LOWER:C_LOWER + P] = np.triu(np.ones((P, P)), 1)
    consts[:, C_CAUSAL:C_CAUSAL + P] = np.triu(np.ones((P, P)))
    consts[:, C_ONES:C_FALL] = 1.0
    consts[:, C_FALL:C_FALL + E1] = np.arange(E1, 0, -1)
    consts[:, C_TILE:C_TILE + FT] = np.arange(FT)
    consts[:, C_BEFORE:CONSTS] = np.where(np.tri(E1, k=-1), -1e-30, 0.0).reshape(-1)

    def columns(*names):
        return np.stack([f[n] for n in names], axis=1)

    ge = lambda w: w.reshape(GROUPS, EPG, P, F0).transpose(2, 0, 1, 3).reshape(P, GROUPS, EPG * F0)
    down = f["L0_ffn_down_w"].reshape(GROUPS, HC, P, P).transpose(2, 0, 1, 3).reshape(P, GROUPS, -1)
    gate_up0 = cat([ge(f["L0_ffn_gate_w"]), ge(f["L0_ffn_up_w"])], axis=2).reshape(P, -1)
    micro = f["L0_ffn_micro_w"].transpose(1, 0, 2).reshape(P, -1)
    pairs = lambda w: w.reshape(PAIRS, 2, P, P).transpose(2, 0, 1, 3).reshape(P, PAIRS, 2 * P)
    w13 = cat([cat([pairs(f["L1_ffn_w1"]), pairs(f["L1_ffn_w3"])], axis=2).reshape(P, -1),
               f["L1_ffn_w1s"][0], f["L1_ffn_w3s"][0], f["L1_ffn_gate_w"].T], axis=1)
    w2 = cat([f["L1_ffn_w2"].transpose(1, 0, 2).reshape(P, -1), f["L1_ffn_w2s"][0]], axis=1)
    arrays = {
        "x": f["L0_attn_x"],
        "consts": consts,
        "router0": cat([f["L0_ffn_macro_w"], micro], axis=1),
        "attn0_w": cat([f["L0_attn_Wg"].T, f["L0_attn_Wv"].T, f["L0_attn_Wd"].T], axis=1),
        "attn0_b": columns("L0_attn_bg", "L0_attn_bv", "L0_attn_bd"),
        "gate_up0": gate_up0,
        "down0": down.reshape(P, -1),
        "attn1_w": cat([f["L1_attn_Wq"].T, f["L1_attn_Wk"].T, f["L1_attn_Wv"]], axis=1),
        "attn1_b": columns("L1_attn_bq", "L1_attn_bk", "L1_attn_bv"),
        "wo1": f["L1_attn_Wo"].T,
        "bo1": np.tile(f["L1_attn_bo"], (P, 1)),
        "w13": w13,
        "w2": w2,
    }
    nc = bacc.Bacc("TRN2", target_bir_lowering=False, num_devices=1)
    named, args = {}, []
    for name, a in arrays.items():
        a = np.ascontiguousarray(a)
        named[f"in_{name}"] = a
        args.append(nc.dram_tensor(f"in_{name}", a.shape, mb.dt.from_np(a.dtype), kind="ExternalInput").ap())
    args.append(nc.dram_tensor("out_x", arrays["x"].shape, mb.dt.from_np(arrays["x"].dtype), kind="ExternalOutput").ap())
    gated_recurrent_moe_two_layers(nc, *args)
    r = run_bass_kernel_spmd(nc, [named], core_ids=[0])
    return r.results[0]["out_x"]
```
